# Optimizing a Trainium2 kernel written in Bass

```python
import numpy as np
import jax
import jax.numpy as jnp

def _softmax(x, axis=-1):
    return jax.nn.softmax(x, axis=axis)

def _gelu(x):
    return jax.nn.gelu(x, approximate=True)

def _silu(x):
    return jax.nn.silu(x)

def _sigmoid(x):
    return jax.nn.sigmoid(x)

def _layernorm(x, axis=-1, eps=1e-05):
    m = jnp.mean(x, axis=axis, keepdims=True)
    v = jnp.var(x, axis=axis, keepdims=True)
    return (x - m) / jnp.sqrt(v + eps)

def _scatter_add(tgt, idx, src, axis=0):
    return tgt.at[idx].add(src)

def _segment_sum(src, seg, n):
    return jax.ops.segment_sum(src, seg, n)
kernel_name = 'mk_gnn_preln_d1_gnn_r8_69c336'

def setup_inputs(seed: int=0):
    np.random.seed(seed)
    _w = jnp.asarray

    def _rec_inputs():
        import jax
        import jax.numpy as jnp
        _gk = jax.random.key(seed)
        x = -0.0003713 + 1 * jax.random.normal(jax.random.fold_in(_gk, 1), (12500, 128), jnp.float32)
        _s = jax.random.randint(jax.random.fold_in(_gk, 2), (100000,), 0, 12500, jnp.int32)
        _d = jax.random.randint(jax.random.fold_in(_gk, 3), (100000,), 0, 12500, jnp.int32)
        _loop = jnp.arange(12500, dtype=jnp.int32)
        src = jnp.concatenate([_s, _d, _loop])
        dst = jnp.concatenate([_d, _s, _loop])
        _o = jnp.argsort(dst, stable=True)
        src = src[_o]
        dst = dst[_o]
        return (x, src, dst)
    x, src, dst = _rec_inputs()

    def _L0_gnn_setup():
        import jax, jax.numpy as jnp
        import numpy as np
        N = 12500
        E = 100000
        IN = 128
        OUT = 128

        def layer_norm(x, g, b, eps=1e-05):
            m = x.mean(-1, keepdims=True)
            v = jnp.mean((x - m) ** 2, axis=-1, keepdims=True)
            return (x - m) * jax.lax.rsqrt(v + eps) * g + b
        key = jax.random.key(seed)
        ks = jax.random.split(key, 8)
        s = 1.0 / np.sqrt(IN)
        x = jax.random.normal(ks[0], (N, IN), jnp.float32)
        edge_index = jax.random.randint(ks[1], (2, E), 0, N)
        batch = jnp.zeros((N,), jnp.int32)
        W1a = jax.random.normal(ks[2], (IN, IN), jnp.float32) * s
        W1b = jax.random.normal(ks[3], (IN, IN), jnp.float32) * s
        ln1_g = jnp.ones((IN,), jnp.float32)
        ln1_b = jnp.zeros((IN,), jnp.float32)
        ln2_g = jnp.ones((IN,), jnp.float32)
        ln2_b = jnp.zeros((IN,), jnp.float32)
        w = jnp.ones((IN,), jnp.float32)
        W2a = jax.random.normal(ks[4], (IN, 2 * IN), jnp.float32) * (1.0 / np.sqrt(2 * IN))
        W2b = jax.random.normal(ks[5], (OUT, IN), jnp.float32) * s
        return {'x': x, 'edge_index': edge_index, 'batch': batch, 'W1a': W1a, 'W1b': W1b, 'ln1_g': ln1_g, 'ln1_b': ln1_b, 'w': w, 'ln2_g': ln2_g, 'ln2_b': ln2_b, 'W2a': W2a, 'W2b': W2b}
    _L0_gnn_all = _L0_gnn_setup()
    _L0_gnn_in = {k: v for k, v in _L0_gnn_all.items() if k in ('W1a', 'W1b', 'ln1_g', 'ln1_b', 'w', 'ln2_g', 'ln2_b', 'W2a', 'W2b')}
    del _L0_gnn_all
    return {'x': x, 'src': src, 'dst': dst, 'L0_gnn_W1a': _L0_gnn_in['W1a'], 'L0_gnn_W1b': _L0_gnn_in['W1b'], 'L0_gnn_ln1_g': _L0_gnn_in['ln1_g'], 'L0_gnn_ln1_b': _L0_gnn_in['ln1_b'], 'L0_gnn_w': _L0_gnn_in['w'], 'L0_gnn_ln2_g': _L0_gnn_in['ln2_g'], 'L0_gnn_ln2_b': _L0_gnn_in['ln2_b'], 'L0_gnn_W2a': _L0_gnn_in['W2a'], 'L0_gnn_W2b': _L0_gnn_in['W2b']}

def reference(x, src, dst, L0_gnn_W1a, L0_gnn_W1b, L0_gnn_ln1_g, L0_gnn_ln1_b, L0_gnn_w, L0_gnn_ln2_g, L0_gnn_ln2_b, L0_gnn_W2a, L0_gnn_W2b):
    import jax
    import jax.numpy as jnp

    def _L0_gnn_ref(x, edge_index, batch, W1a, W1b, ln1_g, ln1_b, w, ln2_g, ln2_b, W2a, W2b):
        import jax, jax.numpy as jnp
        import numpy as np
        N = 12500
        E = 100000
        IN = 128
        OUT = 128

        def layer_norm(x, g, b, eps=1e-05):
            m = x.mean(-1, keepdims=True)
            v = jnp.mean((x - m) ** 2, axis=-1, keepdims=True)
            return (x - m) * jax.lax.rsqrt(v + eps) * g + b
        n = x.shape[0]
        row, col = (edge_index[0], edge_index[1])
        msg = x[row]
        msg = jax.nn.relu(msg @ W1a.T) @ W1b.T
        sums = jax.ops.segment_sum(msg, col, num_segments=n)
        cnt = jax.ops.segment_sum(jnp.ones((msg.shape[0], 1), msg.dtype), col, num_segments=n)
        agg = sums / jnp.maximum(cnt, 1.0)
        agg = layer_norm(agg, ln1_g, ln1_b)
        fx = layer_norm(x + (x - agg) * w, ln2_g, ln2_b)
        out = jnp.concatenate([fx, agg], axis=1)
        return jax.nn.relu(out @ W2a.T) @ W2b.T
    edge_index = jnp.stack([src, dst])
    batch0 = jnp.zeros((12500,), jnp.int32)
    h = jnp.maximum(_layernorm(x, axis=-1), 0.0)
    x = x + _L0_gnn_ref(h, edge_index, batch0, L0_gnn_W1a, L0_gnn_W1b, L0_gnn_ln1_g, L0_gnn_ln1_b, L0_gnn_w, L0_gnn_ln2_g, L0_gnn_ln2_b, L0_gnn_W2a, L0_gnn_W2b)
    return x

_drawn_inputs = setup_inputs


def setup_inputs(seed=0):
    import zlib

    import numpy as np

    out = dict(_drawn_inputs(seed))
    spreads = {'L0_gnn_ln1_g': (1.0, 0.2),
     'L0_gnn_ln1_b': (0.0, 0.1),
     'L0_gnn_w': (1.0, 0.2),
     'L0_gnn_ln2_g': (1.0, 0.2),
     'L0_gnn_ln2_b': (0.0, 0.1)}
    factors = {}
    for name, (base, spread) in spreads.items():
        noise = np.random.default_rng([zlib.crc32(name.encode()), seed]).standard_normal(out[name].shape)
        drawn = base * np.exp(spread * noise) if base else spread * noise
        out[name] = jnp.asarray(drawn.astype(out[name].dtype))
    for name, factor in factors.items():
        out[name] = (out[name] * factor).astype(out[name].dtype)
    return out
```

```python
from contextlib import ExitStack

import concourse.bass as bass
from concourse import mybir

F32 = mybir.dt.float32
I32 = mybir.dt.int32
ALU = mybir.AluOpType
ACT = mybir.ActivationFunctionType
AX = mybir.AxisListType
ds = bass.ds

P = 128
EPS = 1e-5
WIN = 64
BATCH = 7
CHUNKS = ((0, 6), (6, 6), (12, 5))


def gnn_kernel(nc, x, src, dst, W1a, W1b, ln1_g, ln1_b, w, ln2_g, ln2_b, W2a, W2b, out):
    N, D = x.shape
    E, = src.shape
    NT = -(-N // P)
    NPAD = NT * P
    LAST = N - (NT - 1) * P
    ET = -(-E // P)
    TPG = sum(n for _, n in CHUNKS)
    NG = -(-ET // TPG)
    NC = len(CHUNKS)
    EB = -(-ET // P)
    NB = NT // BATCH
    FULL = E // P
    TAIL = E - FULL * P
    ACC = NPAD + P
    assert D == P and NT % BATCH == 0 and NB % 2 == 0 and NG == NT and NG % 2 == 0
    assert CHUNKS[-1][0] + CHUNKS[-1][1] == TPG and N + WIN <= ACC

    table = nc.dram_tensor("messages", [NPAD, D], F32, kind="Internal").ap()
    hT_dram = nc.dram_tensor("h_transposed", [P, NPAD], F32, kind="Internal").ap()

    with ExitStack() as ctx:
        def sb(name, shape, dt=F32):
            return ctx.enter_context(nc.sbuf_tensor(name, shape, dt))

        def sem(name):
            return ctx.enter_context(nc.semaphore(name))

        src_raw = sb("src_raw", [P, EB, P], I32)
        dst_raw = sb("dst_raw", [P, EB, P], I32)
        src_f = sb("src_f", [P, EB, P])
        dst_f = sb("dst_f", [P, EB, P])
        idx = sb("idx", [P, (NG + 1) * TPG], I32)
        dst_t = sb("dst_t", [P, NG * TPG])
        key = sb("key", [P, (NG + 1) * TPG])
        base_b = sb("base_b", [P, NG, NC])
        base_i = sb("base_i", [1, NG * NC], I32)
        least = sb("least", [P, NG])
        slack = sb("slack", [P, NG, NC])
        bad = sb("bad", [P, 4])
        flag_i = sb("flag_i", [1, 1], I32)
        ident = sb("ident", [P, P])
        ones = sb("ones", [P, P])
        win = sb("win", [P, WIN])
        eps = sb("eps", [P, 1])
        w_nat = sb("w_nat", [P, 5, P])
        w_T = sb("w_T", [P, 5, P])
        vec = sb("vec", [P, 5])
        vec2 = sb("vec2", [P, 2])
        diag_h = sb("diag_h", [P, P])
        diag_a = sb("diag_a", [P, P])
        xb = sb("xb", [P, 2, BATCH, D])
        hTb = sb("hTb", [P, 2, BATCH * P])
        st1 = sb("st1", [P, 2, BATCH, 6])
        mean2, apart, spread, apart2, var1 = (sb(n, [P, 2, BATCH]) for n in ("mean2", "apart", "spread", "apart2", "var1"))
        sd1 = sb("sd1", [P, 2, BATCH])
        rs1 = sb("rs1", [P, 2, BATCH])
        nm1 = sb("nm1", [P, 2, BATCH])
        acc = sb("acc", [P, ACC])
        cnt = sb("cnt", [1, ACC])
        idx_now = sb("idx_now", [P, 2, TPG], I32)
        gat = sb("gat", [P, 2, TPG, D])
        early = gat[:, :, :, :].rearrange("p q k d -> p (q k) d")
        hb = early[:, 0:2 * BATCH, :].rearrange("p (q k) d -> p q k d", q=2)
        rb = early[:, 2 * BATCH:4 * BATCH, :].rearrange("p (q k) d -> p q k d", q=2)
        hot = sb("hot", [P, 2, TPG, WIN])
        xn = sb("xn", [P, 2, D])
        hn = sb("hn", [P, 2, P])
        sum_now = sb("sum_now", [P, P])
        cnt_now = sb("cnt_now", [1, P])
        st2 = sb("st2", [P, 6])
        mv2 = sb("mv2", [P, 2])
        small = sb("small", [P, 8])
        z1 = sb("z1", [P, D])
        aT = sb("aT", [P, P])
        st3 = sb("st3", [P, 6])
        mv3 = sb("mv3", [P, 2])
        z2 = sb("z2", [P, D])
        fT = sb("fT", [P, P])
        hid = sb("hid", [P, P])
        res = sb("res", [P, 2, D])
        drow = sb("drow", [1, P], I32)
        gT = sb("gT", [P, P])

        ps = ctx.enter_context(nc.psum_tensor("ps", [P, 8, 512], F32))
        flat = ps[:, :, :].rearrange("p b c -> p (b c)")
        psT = [flat[:, 0:BATCH * P], flat[:, 1024:1024 + BATCH * P]]
        psR = [flat[:, 2048:2048 + BATCH * P], flat[:, 3072:3072 + BATCH * P]]
        psS = [ps[:, 0, 0:NC * WIN], ps[:, 1, 0:NC * WIN]]
        psC = [ps[0:1, 2, 0:NC * WIN], ps[0:1, 3, 0:NC * WIN]]
        pRaw, pCnt, pZ1 = ps[:, 4, 0:D], ps[:, 4, 128:129], ps[:, 4, 256:384]
        pY, pZ2 = ps[:, 5, 0:D], ps[:, 5, 256:384]
        pHid, pOut = ps[:, 6, 0:P], ps[:, 7, 0:D]

        src_pad, dst_pad = sem("src_pad"), sem("dst_pad")
        src_in, dst_in = sem("src_in"), sem("dst_in")
        w_in, vec_in = sem("w_in"), sem("vec_in")
        consts = sem("consts")
        src_cast, dst_cast = sem("src_cast"), sem("dst_cast")
        src_turned, dst_turned = sem("src_turned"), sem("dst_turned")
        idx_zero = sem("idx_zero")
        idx_set, dst_set = sem("idx_set"), sem("dst_set")
        base_sent = sem("base_sent")
        prep = sem("prep")
        bad_set, bad_summed, flag_set = sem("bad_set"), sem("bad_summed"), sem("flag_set")
        w_turned, w_set = sem("w_turned"), sem("w_set")
        vec_set, diag_set = sem("vec_set"), sem("diag_set")
        acc_zero = sem("acc_zero")
        x_in = [sem("x_in0"), sem("x_in1")]
        m_stats, m_joined, m_var, m_std, m_rstd, m_norm = (sem(n) for n in ("m_stats", "m_joined", "m_var", "m_std", "m_rstd", "m_norm"))
        m_h, m_hT, m_hTs, m_r, m_relu = (sem(n) for n in ("m_h", "m_hT", "m_hTs", "m_r", "m_relu"))
        r_out = [sem("r_out0"), sem("r_out1")]
        h_out = [sem("h_out0"), sem("h_out1")]
        idx_ready = sem("idx_ready")
        got = [[sem(f"got{q}_{k}") for k in range(TPG)] for q in range(2)]
        gathers_begun = sem("gathers_begun")
        hot_ready = sem("hot_ready")
        tile_used = sem("tile_used")
        group_used = sem("group_used")
        group_summed = sem("group_summed")
        sums_done, cnts_done = sem("sums_done"), sem("cnts_done")
        xn_in, hn_in = [sem("xn_in0"), sem("xn_in1")], [sem("hn_in0"), sem("hn_in1")]
        u_sums = sem("u_sums")
        u_raw, u_small, u_var, u_std, u_scale, u_z1, u_z1T, u_aT, u_y = (
            sem(n) for n in ("u_raw", "u_small", "u_var", "u_std", "u_scale", "u_z1", "u_z1T", "u_aT", "u_y"))
        u_var2, u_std2, u_scale2, u_z2, u_z2T, u_fT, u_hid, u_hids, u_o, u_res = (
            sem(n) for n in ("u_var2", "u_std2", "u_scale2", "u_z2", "u_z2T", "u_fT", "u_hid", "u_hids", "u_o", "u_res"))
        res_out = [sem("res_out0"), sem("res_out1")]
        g_idx, g_row, g_got, g_turned, g_copied, g_sum, g_cnt = (
            sem(n) for n in ("g_idx", "g_row", "g_got", "g_turned", "g_copied", "g_sum", "g_cnt"))

        vectors = (ln1_g, ln1_b, w, ln2_g, ln2_b)
        weights = (W1a, W1b, W2b, W2a[:, 0:D], W2a[:, D:2 * D])
        W1aT, W1bT, W2bT, W2fT, W2gT = (w_T[:, i, :] for i in range(5))

        block = ctx.enter_context(nc.Block())

        @block.sync
        def _(sp):
            for a, raw, pad, came in ((src, src_raw, src_pad, src_in), (dst, dst_raw, dst_pad, dst_in)):
                full = (EB - 1) * P
                sp.dma_start(raw[:, 0:EB - 1, :],
                             a[0:full * P].rearrange("(b p e) -> p b e", p=P, e=P)).then_inc(came, 16)
                sp.wait_ge(pad, 1)
                sp.dma_start(raw[0:FULL - full, EB - 1, :],
                             a[full * P:FULL * P].rearrange("(p e) -> p e", e=P)).then_inc(came, 16)
                sp.dma_start(raw[FULL - full:FULL - full + 1, EB - 1, 0:TAIL],
                             a[FULL * P:E].rearrange("(p e) -> p e", p=1)).then_inc(came, 16)

            def load_x(i, q, wait):
                if wait:
                    sp.wait_ge(m_h, 2 * i + q - 1)
                sp.dma_start(xb[:, q, :, :], x[ds((2 * i + q) * BATCH * P, BATCH * P), :]
                             .rearrange("(t p) d -> p t d", p=P)).then_inc(x_in[q], 16)

            def store_batch(i, q):
                b = 2 * i + q
                sp.wait_ge(m_hTs, b + 1)
                sp.dma_start(hT_dram[:, ds(b * BATCH * P, BATCH * P)], hTb[:, q, :]).then_inc(h_out[q], 16)
                sp.wait_ge(m_relu, b + 1)
                sp.dma_start(table[ds(b * BATCH * P, BATCH * P), :].rearrange("(t p) d -> p t d", p=P),
                             rb[:, q, :, :]).then_inc(r_out[q], 16)

            load_x(0, 0, False)
            load_x(0, 1, False)
            for k, m in enumerate(weights):
                sp.dma_start(w_nat[:, k, :], m).then_inc(w_in, 16)
            for k, v in enumerate(vectors):
                sp.dma_start(vec[:, k:k + 1], v.rearrange("(p o) -> p o", o=1)).then_inc(vec_in, 16)
            with sp.Fori(0, NB // 2 - 2) as i:
                for q in range(2):
                    load_x(i + 1, q, True)
                    store_batch(i, q)
            i = NB // 2 - 2
            load_x(i + 1, 0, True)
            store_batch(i, 0)
            sp.wait_ge(m_h, NB - 2)
            first = (NB - 1) * BATCH * P
            sp.dma_start(xb[:, 1, 0:BATCH - 1, :], x[first:(NT - 1) * P, :]
                         .rearrange("(t p) d -> p t d", p=P)).then_inc(x_in[1], 16)
            sp.dma_start(xb[0:LAST, 1, BATCH - 1, :], x[(NT - 1) * P:N, :]).then_inc(x_in[1], 16)
            store_batch(i, 1)
            store_batch(i + 1, 0)
            store_batch(i + 1, 1)
            for q in range(2):
                sp.wait_ge(h_out[q], 16 * (NB // 2))

            def load_tile(t, q, last=False):
                rows = LAST if last else P
                sp.dma_start(xn[0:rows, q, :], x[ds(t * P, rows), :]).then_inc(xn_in[q], 16)
                sp.dma_start(hn[:, q, :], hT_dram[:, ds(t * P, P)]).then_inc(hn_in[q], 16)

            def store_tile(t, q, last=False):
                rows = LAST if last else P
                sp.wait_ge(u_res, t + 1)
                sp.dma_start(out[ds(t * P, rows), :], res[0:rows, q, :]).then_inc(res_out[q], 16)

            sp.wait_ge(flag_set, 1)
            flag = sp.value_load(flag_i[0:1, 0:1], min_val=0, max_val=1)
            with sp.If(flag != 0):
                sp.dma_start(drow[:, :], dst[0:P].rearrange("(o e) -> o e", o=1)).then_inc(g_row, 16)
                with sp.Fori(1, FULL) as j:
                    sp.wait_ge(g_sum, j)
                    sp.dma_start(drow[:, :], dst[ds(j * P, P)].rearrange("(o e) -> o e", o=1)).then_inc(g_row, 16)
                sp.wait_ge(g_sum, FULL)
                sp.dma_start(drow[:, 0:TAIL], dst[FULL * P:E].rearrange("(o e) -> o e", o=1)).then_inc(g_row, 16)

            load_tile(0, 0)
            load_tile(1, 1)
            with sp.Fori(0, NT // 2 - 2) as i:
                for q in range(2):
                    store_tile(2 * i + q, q)
                    sp.wait_ge(res_out[q], 16 * (i + 1))
                    load_tile(2 * i + q + 2, q)
            for t in range(NT - 4, NT):
                store_tile(t, t % 2, last=t == NT - 1)
                if t + 2 < NT:
                    sp.wait_ge(res_out[t % 2], 16 * (t // 2 + 1))
                    load_tile(t + 2, t % 2, last=t + 2 == NT - 1)
            for q in range(2):
                sp.wait_ge(res_out[q], 16 * (NT // 2))

        @block.gpsimd
        def _(pool):
            nc.gpsimd.memset(src_raw[:, EB - 1, :], 0).then_inc(src_pad, 1)
            nc.gpsimd.memset(dst_raw[:, EB - 1, :], N).then_inc(dst_pad, 1)
            nc.gpsimd.memset(ident[:, :], 0.0).then_inc(consts, 1)
            pool.wait_ge(consts, 1)
            nc.gpsimd.affine_select(out=ident[:, :], in_=ident[:, :], compare_op=ALU.not_equal, fill=1.0, base=0,
                                    pattern=[[-1, P]], channel_multiplier=1).then_inc(consts, 1)
            nc.gpsimd.memset(ones[:, :], 1.0).then_inc(consts, 1)
            nc.gpsimd.memset(eps[:, :], EPS).then_inc(consts, 1)
            nc.gpsimd.iota(win[:, :], pattern=[[1, WIN]], base=0, channel_multiplier=0,
                           allow_small_or_imprecise_dtypes=True).then_inc(consts, 1)
            nc.gpsimd.iota(least[:, :], pattern=[[P, NG]], base=-P, channel_multiplier=0,
                           allow_small_or_imprecise_dtypes=True).then_inc(consts, 1)
            nc.gpsimd.memset(idx[:, EB * P:], 0).then_inc(consts, 1)
            nc.gpsimd.memset(dst_t[:, EB * P:], float(N)).then_inc(consts, 1)
            nc.gpsimd.memset(key[:, NG * TPG:], 0.0).then_inc(consts, 1)
            nc.gpsimd.memset(acc[:, :], 0.0).then_inc(acc_zero, 1)
            nc.gpsimd.memset(cnt[:, :], 0.0).then_inc(acc_zero, 1)
            pool.wait_ge(flag_set, 1)
            for q in range(2):
                pool.wait_ge(r_out[q], 16 * (NB // 2))
            flag = pool.value_load(flag_i[0:1, 0:1], min_val=0, max_val=1)

            def gather(q, k, index):
                return nc.gpsimd.indirect_dma_start(
                    out=gat[:, q, k, :], out_offset=None, in_=table,
                    in_offset=bass.IndirectOffsetOnAxis(ap=index, axis=0))

            def gather_group(i, q, first):
                pool.wait_ge(idx_ready, 2 * i + q + 1)
                if not first:
                    pool.wait_ge(group_used, 2 * i + q - 1)
                pool.sem_inc(gathers_begun, 1)
                for k in range(TPG):
                    gather(q, k, idx_now[:, q, k:k + 1]).then_inc(got[q][k], 16)

            with pool.If(flag == 0):
                for q in range(2):
                    gather_group(0, q, True)
                with pool.Fori(1, NG // 2) as i:
                    for q in range(2):
                        gather_group(i, q, False)
            with pool.Else():
                def gather_tile(j, first):
                    pool.wait_ge(g_idx, j + 1)
                    if not first:
                        pool.wait_ge(g_turned, j)
                    pool.sem_inc(gathers_begun, 1)
                    gather(0, 0, idx_now[:, 0, 0:1]).then_inc(g_got, 16)

                gather_tile(0, True)
                with pool.Fori(1, ET) as j:
                    gather_tile(j, False)

        @block.tensor
        def _(pe):
            pe.wait_ge(consts, 9)
            for n, (f, cast, turned, free) in enumerate(((src_f, src_cast, src_turned, None),
                                                         (dst_f, dst_cast, dst_turned, idx_set))):
                pe.wait_ge(cast, 1)
                if free is not None:
                    pe.wait_ge(free, 1)
                for b in range(EB):
                    last = nc.tensor.transpose(flat[:, b * P:(b + 1) * P], f[:, b, :], ident[:, :])
                last.then_inc(turned, 1)
            pe.wait_ge(w_in, 16 * len(weights))
            for k in range(len(weights)):
                last = nc.tensor.transpose(flat[:, 2048 + k * P:2048 + (k + 1) * P], w_nat[:, k, :], ident[:, :])
            last.then_inc(w_turned, 1)
            pe.wait_ge(dst_set, 1)
            for c, (first, _) in enumerate(CHUNKS):
                last = nc.tensor.matmul(ps[:, 6, c * NG:(c + 1) * NG], ones[0:1, :],
                                        dst_t[0:1, first:NG * TPG:TPG], start=True, stop=True)
            last.then_inc(base_sent, 1)
            pe.wait_ge(bad_set, 1)
            nc.tensor.matmul(ps[0:1, 7, 0:1], ones[:, 0:1], bad[:, 3:4], start=True, stop=True).then_inc(bad_summed, 1)
            pe.wait_ge(w_set, 1)
            pe.wait_ge(flag_set, 1)

            def turn_h(i, q):
                b = 2 * i + q
                pe.wait_ge(m_h, b + 1)
                if not (isinstance(i, int) and b < 2):
                    pe.wait_ge(m_hTs, b - 1)
                for k in range(BATCH):
                    last = nc.tensor.transpose(psT[q][:, k * P:(k + 1) * P], hb[:, q, k, :], ident[:, :])
                last.then_inc(m_hT, 1)

            def multiply_h(i, q):
                b = 2 * i + q
                pe.wait_ge(m_hTs, b + 1)
                if not (isinstance(i, int) and b < 2):
                    pe.wait_ge(m_relu, b - 1)
                for k in range(BATCH):
                    last = nc.tensor.matmul(psR[q][:, k * P:(k + 1) * P], hTb[:, q, k * P:(k + 1) * P], W1aT,
                                            start=True, stop=True)
                last.then_inc(m_r, 1)

            for q in range(2):
                turn_h(0, q)
                multiply_h(0, q)
            with pe.Fori(1, NB // 2) as i:
                for q in range(2):
                    turn_h(i, q)
                    multiply_h(i, q)
            pe.wait_ge(m_relu, NB)
            pe.wait_ge(diag_set, 2)
            pe.wait_ge(acc_zero, 2)

            def raw(t, q):
                pe.wait_ge(u_sums, 2 * t + 2)
                nc.tensor.matmul(pRaw, sum_now[:, :], W1bT, start=True, stop=True)
                nc.tensor.matmul(pCnt, cnt_now[:, :], ones[0:1, 0:1], start=True, stop=True).then_inc(u_raw, 1)

            def turn_agg(t, q):
                pe.wait_ge(u_z1, t + 1)
                nc.tensor.transpose(pZ1, z1[:, :], ident[:, :]).then_inc(u_z1T, 1)

            def mix(t, q, i):
                pe.wait_ge(u_aT, t + 1)
                pe.wait_ge(hn_in[q], 16 * (i + 1))
                nc.tensor.matmul(pY, hn[:, q, :], diag_h[:, :], start=True, stop=False)
                nc.tensor.matmul(pY, aT[:, :], diag_a[:, :], start=False, stop=True).then_inc(u_y, 1)

            def turn_fx(t, q):
                pe.wait_ge(u_z2, t + 1)
                nc.tensor.transpose(pZ2, z2[:, :], ident[:, :]).then_inc(u_z2T, 1)

            def hidden(t, q):
                pe.wait_ge(u_fT, t + 1)
                nc.tensor.matmul(pHid, W2fT, fT[:, :], start=True, stop=False)
                nc.tensor.matmul(pHid, W2gT, aT[:, :], start=False, stop=True).then_inc(u_hid, 1)

            def project(t, q):
                pe.wait_ge(u_hids, t + 1)
                nc.tensor.matmul(pOut, hid[:, :], W2bT, start=True, stop=True).then_inc(u_o, 1)

            def step(k, i, q):
                t = 2 * i + q
                if k == 0:
                    raw(t, q)
                if k == 2:
                    turn_agg(t, q)
                if k == 5:
                    mix(t, q, i)
                if k == 8:
                    turn_fx(t, q)
                if k == 11:
                    hidden(t, q)
                if k == 14:
                    project(t, q)

            def group(i, q, first):
                g = 2 * i + q
                pe.wait_ge(hot_ready, g + 1)
                if not first:
                    pe.wait_ge(sums_done, NC * (g - 1))
                    pe.wait_ge(cnts_done, NC * (g - 1))
                for c, (k0, n) in enumerate(CHUNKS):
                    for k in range(k0, k0 + n):
                        pe.wait_ge(got[q][k], 16 * (i + 1))
                        nc.tensor.matmul(psS[q][:, c * WIN:(c + 1) * WIN], gat[:, q, k, :], hot[:, q, k, :],
                                         start=k == k0, stop=k == k0 + n - 1)
                        last = nc.tensor.matmul(psC[q][:, c * WIN:(c + 1) * WIN], ones[:, 0:1], hot[:, q, k, :],
                                                start=k == k0, stop=k == k0 + n - 1)
                        if k == TPG - 1:
                            last.then_inc(group_used, 1)
                        if not first:
                            step(k, i - 1, q)

            flag = pe.value_load(flag_i[0:1, 0:1], min_val=0, max_val=1)
            with pe.If(flag == 0):
                for q in range(2):
                    group(0, q, True)
                with pe.Fori(1, NG // 2) as i:
                    for q in range(2):
                        group(i, q, False)
                for q in range(2):
                    for k in range(TPG):
                        step(k, NT // 2 - 1, q)
            with pe.Else():
                def turn_tile(j, first):
                    pe.wait_ge(g_got, 16 * (j + 1))
                    if not first:
                        pe.wait_ge(g_copied, j)
                    nc.tensor.transpose(ps[:, 0, 0:P], gat[:, 0, 0, :], ident[:, :]).then_inc(g_turned, 1)

                turn_tile(0, True)
                with pe.Fori(1, ET) as j:
                    turn_tile(j, False)
                with pe.Fori(0, NT // 2) as i:
                    for q in range(2):
                        for k in range(TPG):
                            step(k, i, q)

        @block.scalar
        def _(act):
            act.wait_ge(consts, 9)

            def std(i, q):
                b = 2 * i + q
                act.wait_ge(m_var, b + 1)
                nc.scalar.activation(sd1[:, q, :], var1[:, q, :], ACT.Sqrt, bias=eps[:, 0:1]).then_inc(m_std, 1)

            def normalise(i, q):
                b = 2 * i + q
                act.wait_ge(m_norm, b + 1)
                if not (isinstance(i, int) and b < 2):
                    act.wait_ge(m_hT, b - 1)
                for k in range(BATCH):
                    last = nc.scalar.activation(hb[:, q, k, :], xb[:, q, k, :], ACT.Relu,
                                                scale=rs1[:, q, k:k + 1], bias=nm1[:, q, k:k + 1])
                last.then_inc(m_h, 1)

            def relu(i, q):
                b = 2 * i + q
                act.wait_ge(m_r, b + 1)
                if not (isinstance(i, int) and b < 2):
                    act.wait_ge(r_out[q], 16 * i)
                nc.scalar.activation(rb[:, q, :, :].rearrange("p t d -> p (t d)"), psR[q], ACT.Relu).then_inc(m_relu, 1)

            std(0, 0)
            normalise(0, 0)
            std(0, 1)
            normalise(0, 1)
            relu(0, 0)
            std(1, 0)
            normalise(1, 0)
            relu(0, 1)
            with act.Fori(1, NB // 2 - 1) as i:
                std(i, 1)
                normalise(i, 1)
                relu(i, 0)
                std(i + 1, 0)
                normalise(i + 1, 0)
                relu(i, 1)
            i = NB // 2 - 1
            std(i, 1)
            normalise(i, 1)
            relu(i, 0)
            relu(i, 1)

            act.wait_ge(vec_in, 16 * len(vectors))
            with act.Fori(0, NT) as t:
                act.wait_ge(u_small, 3 * t + 3)
                nc.scalar.activation(small[:, 3:4], small[:, 2:3], ACT.Sqrt).then_inc(u_std, 1)
                act.wait_ge(u_z1T, t + 1)
                nc.scalar.activation(aT[:, :], pZ1, ACT.Identity, scale=vec[:, 0:1], bias=vec[:, 1:2]).then_inc(u_aT, 1)
                act.wait_ge(u_var2, t + 1)
                nc.scalar.activation(small[:, 5:6], mv3[:, 1:2], ACT.Sqrt, bias=eps[:, 0:1]).then_inc(u_std2, 1)
                act.wait_ge(u_z2T, t + 1)
                nc.scalar.activation(fT[:, :], pZ2, ACT.Identity, scale=vec[:, 3:4], bias=vec[:, 4:5]).then_inc(u_fT, 1)
                act.wait_ge(u_hid, t + 1)
                nc.scalar.activation(hid[:, :], pHid, ACT.Relu).then_inc(u_hids, 1)

        @block.vector
        def _(dve):
            dve.wait_ge(consts, 9)
            dve.wait_ge(src_in, 48)
            nc.vector.tensor_copy(src_f[:, :, :], src_raw[:, :, :]).then_inc(src_cast, 1)
            dve.wait_ge(dst_in, 48)
            nc.vector.tensor_copy(dst_f[:, :, :], dst_raw[:, :, :]).then_inc(dst_cast, 1)
            dve.wait_ge(src_turned, 1)
            nc.vector.tensor_copy(idx[:, 0:EB * P], flat[:, 0:EB * P]).then_inc(idx_set, 1)
            dve.wait_ge(dst_turned, 1)
            nc.vector.tensor_copy(dst_t[:, 0:EB * P], flat[:, 0:EB * P]).then_inc(dst_set, 1)
            dve.wait_ge(w_turned, 1)
            nc.vector.tensor_copy(w_T[:, :, :].rearrange("p k d -> p (k d)"),
                                  flat[:, 2048:2048 + 5 * P]).then_inc(w_set, 1)
            dve.wait_ge(vec_in, 16 * len(vectors))
            nc.vector.tensor_scalar(vec2[:, 0:1], vec[:, 2:3], 1.0, None, ALU.add).then_inc(vec_set, 1)
            nc.vector.tensor_scalar(vec2[:, 1:2], vec[:, 2:3], -1.0, None, ALU.mult).then_inc(vec_set, 1)
            dve.wait_ge(vec_set, 2)
            nc.vector.tensor_scalar(diag_h[:, :], ident[:, :], vec2[:, 0:1], None, ALU.mult).then_inc(diag_set, 1)
            nc.vector.tensor_scalar(diag_a[:, :], ident[:, :], vec2[:, 1:2], None, ALU.mult).then_inc(diag_set, 1)
            dve.wait_ge(base_sent, 1)
            nc.vector.tensor_copy(base_b[:, :, :].rearrange("p g c -> p c g"),
                                  ps[:, 6, 0:NC * NG].rearrange("p (c g) -> p c g", c=NC)).then_inc(prep, 1)
            dve.wait_ge(prep, 1)
            dve.wait_ge(dst_set, 1)
            nc.vector.tensor_copy(base_i[:, :], base_b[0:1, :, :].rearrange("p g c -> p (g c)")).then_inc(prep, 1)
            by_group = lambda a: a[:, 0:NG * TPG].rearrange("p (g k) -> p g k", k=TPG)
            for c, (k0, n) in enumerate(CHUNKS):
                nc.vector.tensor_tensor(by_group(key)[:, :, k0:k0 + n], by_group(dst_t)[:, :, k0:k0 + n],
                                        base_b[:, :, c:c + 1].broadcast_to([P, NG, n]), ALU.subtract).then_inc(prep, 1)
            nc.vector.tensor_tensor(slack[:, :, :], base_b[:, :, :],
                                    least[:, :].unsqueeze(2).broadcast_to([P, NG, NC]), ALU.subtract).then_inc(prep, 1)
            dve.wait_ge(prep, 6)
            nc.vector.tensor_reduce(bad[:, 0:1], key[:, 0:NG * TPG], AX.X, ALU.max).then_inc(prep, 1)
            nc.vector.tensor_reduce(bad[:, 1:2], key[:, 0:NG * TPG], AX.X, ALU.min).then_inc(prep, 1)
            nc.vector.tensor_reduce(bad[:, 2:3], slack[:, :, :], AX.XY, ALU.min).then_inc(prep, 1)
            dve.wait_ge(prep, 9)
            nc.vector.tensor_scalar(bad[:, 3:4], bad[:, 0:1], float(WIN), None, ALU.is_ge).then_inc(prep, 1)
            for m in (1, 2):
                dve.wait_ge(prep, 9 + m)
                last = nc.vector.scalar_tensor_tensor(out=bad[:, 3:4], in0=bad[:, m:m + 1], scalar=0.0,
                                                      in1=bad[:, 3:4], op0=ALU.is_lt, op1=ALU.add)
                last.then_inc(prep if m == 1 else bad_set, 1)
            dve.wait_ge(bad_summed, 1)
            nc.vector.tensor_scalar(flag_i[:, :], ps[0:1, 7, 0:1], 1.0, None, ALU.min).then_inc(flag_set, 1)

            def stats(i, q, extra=0):
                b = 2 * i + q
                dve.wait_ge(x_in[q], 16 * (i + 1) + extra)
                for k in range(BATCH):
                    last = nc.vector.bn_stats(st1[:, q, k, :], xb[:, q, k, :])
                last.then_inc(m_stats, 1)
                dve.wait_ge(m_stats, b + 1)
                ev, od = st1[:, q, :, 0:3], st1[:, q, :, 3:6]
                nc.vector.tensor_tensor(mean2[:, q, :], ev[:, :, 1], od[:, :, 1], ALU.add)
                nc.vector.tensor_tensor(apart[:, q, :], ev[:, :, 1], od[:, :, 1], ALU.subtract)
                nc.vector.tensor_tensor(spread[:, q, :], ev[:, :, 2], od[:, :, 2], ALU.add).then_inc(m_joined, 1)
                dve.wait_ge(m_joined, 2 * b + 1)
                nc.vector.scalar_tensor_tensor(out=apart2[:, q, :], in0=apart[:, q, :], scalar=0.25, in1=apart[:, q, :],
                                               op0=ALU.mult, op1=ALU.mult).then_inc(m_joined, 1)
                dve.wait_ge(m_joined, 2 * b + 2)
                nc.vector.scalar_tensor_tensor(out=var1[:, q, :], in0=spread[:, q, :], scalar=1.0 / D, in1=apart2[:, q, :],
                                               op0=ALU.mult, op1=ALU.add).then_inc(m_var, 1)
                dve.wait_ge(m_std, b + 1)
                if not (isinstance(i, int) and b < 2):
                    dve.wait_ge(m_h, b - 1)
                nc.vector.reciprocal(rs1[:, q, :], sd1[:, q, :]).then_inc(m_rstd, 1)
                dve.wait_ge(m_rstd, b + 1)
                nc.vector.scalar_tensor_tensor(out=nm1[:, q, :], in0=mean2[:, q, :], scalar=-0.5, in1=rs1[:, q, :],
                                               op0=ALU.mult, op1=ALU.mult).then_inc(m_norm, 1)

            def keep_h(i, q):
                b = 2 * i + q
                dve.wait_ge(m_hT, b + 1)
                if not (isinstance(i, int) and b < 2):
                    dve.wait_ge(h_out[q], 16 * i)
                    dve.wait_ge(m_r, b - 1)
                nc.vector.tensor_copy(hTb[:, q, :], psT[q]).then_inc(m_hTs, 1)

            stats(0, 0)
            stats(0, 1)
            keep_h(0, 0)
            stats(1, 0)
            keep_h(0, 1)
            with dve.Fori(1, NB // 2 - 1) as i:
                stats(i, 1)
                keep_h(i, 0)
                stats(i + 1, 0)
                keep_h(i, 1)
            i = NB // 2 - 1
            stats(i, 1, extra=16)
            keep_h(i, 0)
            keep_h(i, 1)

            def ready_group(i, q, first):
                g = 2 * i + q
                if not first:
                    dve.wait_ge(group_used, g - 1)
                nc.vector.tensor_copy(idx_now[:, q, :], idx[:, ds(g * TPG, TPG)]).then_inc(idx_ready, 1)
                nc.vector.tensor_tensor(hot[:, q, :, :], win[:, :].unsqueeze(1).broadcast_to([P, TPG, WIN]),
                                        key[:, ds(g * TPG, TPG)].unsqueeze(2).broadcast_to([P, TPG, WIN]),
                                        ALU.is_equal).then_inc(hot_ready, 1)

            def add_group(i, q):
                g = 2 * i + q
                dve.wait_ge(group_used, g + 1)
                for c in range(NC):
                    at = dve.value_load(base_i[0:1, ds(g * NC + c, 1)], min_val=0, max_val=N)
                    dve.wait_ge(sums_done, g * NC + c)
                    nc.vector.tensor_tensor(acc[:, ds(at, WIN)], acc[:, ds(at, WIN)],
                                            psS[q][:, c * WIN:(c + 1) * WIN], ALU.add).then_inc(sums_done, 1)
                    dve.wait_ge(cnts_done, g * NC + c)
                    nc.vector.tensor_tensor(cnt[:, ds(at, WIN)], cnt[:, ds(at, WIN)],
                                            psC[q][:, c * WIN:(c + 1) * WIN], ALU.add).then_inc(cnts_done, 1)

            def update(i, q):
                t = 2 * i + q
                nc.vector.tensor_copy(sum_now[:, :], acc[:, ds(t * P, P)]).then_inc(u_sums, 1)
                nc.vector.tensor_copy(cnt_now[:, :], cnt[:, ds(t * P, P)]).then_inc(u_sums, 1)
                dve.wait_ge(u_raw, t + 1)
                nc.vector.bn_stats(st2[:, :], pRaw)
                nc.vector.tensor_scalar(small[:, 0:1], pCnt, 1.0, None, ALU.max).then_inc(u_small, 1)
                dve.wait_ge(u_small, 3 * t + 1)
                nc.vector.scalar_tensor_tensor(out=small[:, 1:2], in0=small[:, 0:1], scalar=EPS, in1=small[:, 0:1],
                                               op0=ALU.mult, op1=ALU.mult).then_inc(u_small, 1)
                dve.drain()
                nc.vector.bn_aggr(mv2[:, :], st2[:, :]).then_inc(u_var, 1)
                dve.wait_ge(u_small, 3 * t + 2)
                dve.wait_ge(u_var, t + 1)
                nc.vector.tensor_tensor(small[:, 2:3], small[:, 1:2], mv2[:, 1:2], ALU.add).then_inc(u_small, 1)
                dve.wait_ge(u_std, t + 1)
                nc.vector.reciprocal(small[:, 4:5], small[:, 3:4]).then_inc(u_scale, 1)
                dve.wait_ge(u_scale, t + 1)
                nc.vector.tensor_scalar(z1[:, :], pRaw, mv2[:, 0:1], small[:, 4:5],
                                        ALU.subtract, ALU.mult).then_inc(u_z1, 1)
                dve.wait_ge(u_y, t + 1)
                nc.vector.bn_stats(st3[:, :], pY)
                dve.drain()
                nc.vector.bn_aggr(mv3[:, :], st3[:, :]).then_inc(u_var2, 1)
                dve.wait_ge(u_std2, t + 1)
                nc.vector.reciprocal(small[:, 6:7], small[:, 5:6]).then_inc(u_scale2, 1)
                dve.wait_ge(u_scale2, t + 1)
                dve.wait_ge(u_var2, t + 1)
                nc.vector.tensor_scalar(z2[:, :], pY, mv3[:, 0:1], small[:, 6:7],
                                        ALU.subtract, ALU.mult).then_inc(u_z2, 1)
                dve.wait_ge(u_o, t + 1)
                dve.wait_ge(xn_in[q], 16 * (i + 1))
                nc.vector.tensor_tensor(res[:, q, :], pOut, xn[:, q, :], ALU.add).then_inc(u_res, 1)

            dve.wait_ge(acc_zero, 2)
            flag = dve.value_load(flag_i[0:1, 0:1], min_val=0, max_val=1)
            with dve.If(flag == 0):
                ready_group(0, 0, True)
                ready_group(0, 1, True)
                add_group(0, 0)
                ready_group(1, 0, False)
                add_group(0, 1)
                with dve.Fori(1, NG // 2) as i:
                    for q in range(2):
                        ready_group(i + q, 1 - q, False)
                        dve.wait_ge(sums_done, NC * (2 * i + q))
                        dve.wait_ge(cnts_done, NC * (2 * i + q))
                        update(i - 1, q)
                        add_group(i, q)
                dve.wait_ge(sums_done, NC * NG)
                dve.wait_ge(cnts_done, NC * NG)
                for q in range(2):
                    update(NT // 2 - 1, q)
            with dve.Else():
                def add_edges(j, n):
                    dve.wait_ge(g_row, 16 * (j + 1))
                    dve.wait_ge(g_turned, j + 1)
                    nc.vector.tensor_copy(gT[:, :], ps[:, 0, 0:P]).then_inc(g_copied, 1)
                    dve.drain()
                    with dve.Fori(0, n) as e:
                        at = dve.value_load(drow[0:1, ds(e, 1)], min_val=0, max_val=N - 1)
                        nc.vector.tensor_tensor(acc[:, ds(at, 1)], acc[:, ds(at, 1)], gT[:, ds(e, 1)], ALU.add)
                        nc.vector.tensor_tensor(cnt[:, ds(at, 1)], cnt[:, ds(at, 1)], ones[0:1, 0:1], ALU.add)
                        dve.drain()
                    dve.drain().then_inc(g_sum, 1)

                with dve.Fori(0, FULL) as j:
                    nc.vector.tensor_copy(idx_now[:, 0, 0:1], idx[:, ds(j, 1)]).then_inc(g_idx, 1)
                    add_edges(j, P)
                nc.vector.tensor_copy(idx_now[:, 0, 0:1], idx[:, FULL:FULL + 1]).then_inc(g_idx, 1)
                add_edges(FULL, TAIL)
                dve.wait_ge(g_sum, ET)
                with dve.Fori(0, NT // 2) as i:
                    for q in range(2):
                        update(i, q)


_INS = ['x', 'src', 'dst', 'L0_gnn_W1a', 'L0_gnn_W1b', 'L0_gnn_ln1_g', 'L0_gnn_ln1_b', 'L0_gnn_w', 'L0_gnn_ln2_g',
        'L0_gnn_ln2_b', 'L0_gnn_W2a', 'L0_gnn_W2b']


def kernel(**inputs):
    import numpy as _np
    import concourse.bacc as _bacc
    from concourse import mybir as _mybir
    from concourse.bass_utils import run_bass_kernel_spmd as _run

    nc = _bacc.Bacc("TRN2", target_bir_lowering=False, num_devices=1)
    arrays, args = {}, []
    for name in _INS:
        a = _np.ascontiguousarray(inputs[name])
        arrays[f"in_{name}_dram"] = a
        args.append(nc.dram_tensor(f"in_{name}_dram", a.shape, _mybir.dt.from_np(a.dtype), kind="ExternalInput").ap())
    out = nc.dram_tensor("out_0_dram", inputs['x'].shape, _mybir.dt.float32, kind="ExternalOutput").ap()
    gnn_kernel(nc, *args, out)
    r = _run(nc, [arrays], core_ids=[0])
    return r.results[0]["out_0_dram"]
```

```python
from contextlib import ExitStack

import concourse.bass as bass
from concourse import mybir

F32 = mybir.dt.float32
I32 = mybir.dt.int32
ALU = mybir.AluOpType
ACT = mybir.ActivationFunctionType
AX = mybir.AxisListType
ds = bass.ds

P = 128
EPS = 1e-5
WIN = 64
BATCH = 7
CHUNKS = ((0, 6), (6, 6), (12, 5))


def gnn_kernel(nc, x, src, dst, W1a, W1b, ln1_g, ln1_b, w, ln2_g, ln2_b, W2a, W2b, out):
    N, D = x.shape
    E, = src.shape
    NT = -(-N // P)
    NPAD = NT * P
    LAST = N - (NT - 1) * P
    ET = -(-E // P)
    TPG = sum(n for _, n in CHUNKS)
    NG = -(-ET // TPG)
    NC = len(CHUNKS)
    EB = -(-ET // P)
    NB = NT // BATCH
    FULL = E // P
    TAIL = E - FULL * P
    LASTK = ET - (NG - 1) * TPG
    RAW = TPG - 1
    NR = NG - 1
    NR0 = 6
    ACC = max(NPAD, N + WIN)
    assert D == P and NT % BATCH == 0 and NB % 2 == 0 and NG == NT and NG % 2 == 0
    assert LASTK < TPG and [c for c in CHUNKS if c[0] < LASTK] == [c for c in CHUNKS if sum(c) <= LASTK]
    assert CHUNKS[-1][0] + CHUNKS[-1][1] == TPG and N + WIN <= ACC

    table = nc.dram_tensor("messages", [NPAD, D], F32, kind="Internal").ap()

    with ExitStack() as ctx:
        def sb(name, shape, dt=F32):
            return ctx.enter_context(nc.sbuf_tensor(name, shape, dt))

        def sem(name):
            return ctx.enter_context(nc.semaphore(name))

        acc = sb("acc", [P, ACC])
        cnt_rows = sb("cnt_rows", [P, ACC])
        cnt = cnt_rows[0:1, :]
        x_src = sb("x_src", [P, NR, D])
        gat = sb("gat", [P, 2, TPG, D])
        hot = sb("hot", [P, 2, TPG, WIN])
        hot_sum = sb("hot_sum", [P, 2, NC, WIN])
        idx_now = sb("idx_now", [P, 2, TPG], I32)
        idx_first = sb("idx_first", [P, NR0], I32)

        def early(whole, at, *shape):
            size = 1
            for n in shape:
                size *= n
            a = whole[:, at:at + size]
            names = "abc"[:len(shape)]
            return a.rearrange(f"p ({' '.join(names)}) -> p {' '.join(names)}", **dict(zip(names, shape)))

        src_raw = early(acc, 0, EB, P).bitcast(I32)
        dst_raw = early(acc, EB * P, EB, P).bitcast(I32)
        src_f = early(acc, 2 * EB * P, EB, P)
        dst_f = early(acc, 3 * EB * P, EB, P)
        xb = early(cnt_rows, 0, 2, BATCH, D)
        hb = early(cnt_rows, 2 * BATCH * D, 2, BATCH, D)
        rb = early(cnt_rows, 4 * BATCH * D, 2, BATCH, D)
        hTb = early(cnt_rows, 6 * BATCH * D, 2, BATCH * P)
        idx = sb("idx", [P, (NG + 1) * TPG], I32)
        key = sb("key", [P, (NG + 1) * TPG])
        base_b = early(acc, 5 * EB * P + 5 * P, NG, NC)
        base_i = sb("base_i", [1, NG * NC], I32)
        least = early(acc, 4 * EB * P, NG)
        slack = early(acc, 4 * EB * P + NG, NG, NC)
        bad = sb("bad", [P, 4])
        flag_i = sb("flag_i", [1, 1], I32)
        ident = sb("ident", [P, P])
        ones = sb("ones", [P, P])
        win = sb("win", [P, WIN])
        eps = sb("eps", [P, 1])
        w_nat = early(acc, 5 * EB * P, 5, P)
        w_T = sb("w_T", [P, 5, P])
        vec = sb("vec", [P, 5])
        vec2 = sb("vec2", [P, 2])
        diag_h = sb("diag_h", [P, P])
        diag_a = sb("diag_a", [P, P])
        st1 = sb("st1", [P, 2, BATCH, 6])
        mean2, apart, spread, apart2, var1, sd1 = (
            sb(n, [P, 2, BATCH]) for n in ("mean2", "apart", "spread", "apart2", "var1", "sd1"))
        rs1 = sb("rs1", [P, 2, BATCH])
        nm1 = sb("nm1", [P, 2, BATCH])
        rs_all = sb("rs_all", [P, NT])
        nm_all = sb("nm_all", [P, NT])
        e_st = sb("e_st", [P, 6])
        e_mv = sb("e_mv", [P, 2])
        e_sc = sb("e_sc", [P, 3])
        e_h = sb("e_h", [P, D])
        e_hT = sb("e_hT", [P, P])
        xn = sb("xn", [P, 2, D])
        hn = sb("hn", [P, 2, D])
        hT = sb("hT", [P, 2, P])
        sum_now = sb("sum_now", [P, 2, P])
        cnt_now = sb("cnt_now", [1, 2, P])
        st2 = sb("st2", [P, 2, 6])
        mv2 = sb("mv2", [P, 2, 2])
        small = sb("small", [P, 2, 8])
        z1 = sb("z1", [P, 2, D])
        aT = sb("aT", [P, 2, P])
        st3 = sb("st3", [P, 2, 6])
        mv3 = sb("mv3", [P, 2, 2])
        z2 = sb("z2", [P, 2, D])
        fT = sb("fT", [P, 2, P])
        hid = sb("hid", [P, 2, P])
        res = sb("res", [P, 2, D])
        drow = e_h[0:1, :].bitcast(I32)
        gT = e_hT

        ps = ctx.enter_context(nc.psum_tensor("ps", [P, 8, 512], F32))
        flat = ps[:, :, :].rearrange("p b c -> p (b c)")
        psT = [flat[:, 0:BATCH * P], flat[:, 1024:1024 + BATCH * P]]
        psR = [flat[:, 2048:2048 + BATCH * P], flat[:, 3072:3072 + BATCH * P]]
        psS = [ps[:, q, 0:NC * WIN] for q in range(2)]
        psC = [ps[0:1, q, 256:256 + NC * WIN] for q in range(2)]
        pEh, pEr = ps[:, 2, 0:P], ps[:, 2, 128:256]
        pSum, pY, pOut = ([ps[:, 3 + q, a:a + P] for q in range(2)] for a in (0, 128, 256))
        pCnt = [ps[:, 3 + q, 384:385] for q in range(2)]
        pH, pZ1, pZ2, pHid = ([ps[:, 5 + q, a:a + P] for q in range(2)] for a in (0, 128, 256, 384))

        src_pad, dst_pad = sem("src_pad"), sem("dst_pad")
        src_in, dst_in = sem("src_in"), sem("dst_in")
        w_in, vec_in = sem("w_in"), sem("vec_in")
        ident_zero, consts = sem("ident_zero"), sem("consts")
        src_cast, dst_cast = sem("src_cast"), sem("dst_cast")
        src_turned, dst_turned = sem("src_turned"), sem("dst_turned")
        idx_set, dst_set = sem("idx_set"), sem("dst_set")
        base_sent = sem("base_sent")
        prep = sem("prep")
        bad_set, bad_summed, flag_set = sem("bad_set"), sem("bad_summed"), sem("flag_set")
        w_turned, w_set = sem("w_turned"), sem("w_set")
        vec_set, diag_set = sem("vec_set"), sem("diag_set")
        acc_zero = sem("acc_zero")
        x_in = [sem("x_in0"), sem("x_in1")]
        m_stats, m_joined, m_var, m_std, m_rstd, m_norm = (sem(n) for n in ("m_stats", "m_joined", "m_var", "m_std", "m_rstd", "m_norm"))
        m_h, m_hT, m_hTs, m_r, m_relu = (sem(n) for n in ("m_h", "m_hT", "m_hTs", "m_r", "m_relu"))
        r_out = [sem("r_out0"), sem("r_out1")]
        idx_ready = sem("idx_ready")
        got = [[sem(f"got{q}_{k}") for k in range(TPG)] for q in range(2)]
        gathers_begun = sem("gathers_begun")
        hot_made = sem("hot_made")
        hot_ready = sem("hot_ready")
        group_used = sem("group_used")
        sums_done, cnts_done = sem("sums_done"), sem("cnts_done")
        xn_in = [sem("xn_in0"), sem("xn_in1")]
        first_in, x_src_in = sem("first_in"), sem("x_src_in")
        e_var, e_std, e_rstd, e_norm, e_hs, e_turned, e_copied, e_made, e_msg = (
            sem(n) for n in ("e_var", "e_std", "e_rstd", "e_norm", "e_hs", "e_turned", "e_copied", "e_made", "e_msg"))
        u_h, u_hT, u_hTs = sem("u_h"), sem("u_hT"), sem("u_hTs")
        u_sums = sem("u_sums")
        u_raw, u_small, u_var, u_std, u_scale, u_z1, u_z1T, u_aT, u_y = (
            sem(n) for n in ("u_raw", "u_small", "u_var", "u_std", "u_scale", "u_z1", "u_z1T", "u_aT", "u_y"))
        u_var2, u_std2, u_scale2, u_z2, u_z2T, u_fT, u_hid, u_hids, u_o, u_res = (
            sem(n) for n in ("u_var2", "u_std2", "u_scale2", "u_z2", "u_z2T", "u_fT", "u_hid", "u_hids", "u_o", "u_res"))
        res_out = [sem("res_out0"), sem("res_out1")]
        g_idx, g_row, g_got, g_turned, g_copied, g_sum, g_cnt = (
            sem(n) for n in ("g_idx", "g_row", "g_got", "g_turned", "g_copied", "g_sum", "g_cnt"))

        vectors = (ln1_g, ln1_b, w, ln2_g, ln2_b)
        weights = (W1a, W1b, W2b, W2a[:, 0:D], W2a[:, D:2 * D])
        W1aT, W1bT, W2bT, W2fT, W2gT = (w_T[:, i, :] for i in range(5))

        block = ctx.enter_context(nc.Block())

        @block.sync
        def _(sp):
            sp.dma_start(idx_first[:, :], src[0:NR0 * TPG * P].rearrange("(g k p) -> p g k", k=TPG, p=P)[:, :, RAW],
                         allow_slow_non_contiguous=True).then_inc(first_in, 16)

            def load_edges(a, raw, pad, came):
                full = (EB - 1) * P
                sp.dma_start(raw[:, 0:EB - 1, :],
                             a[0:full * P].rearrange("(b p e) -> p b e", p=P, e=P)).then_inc(came, 16)
                sp.wait_ge(pad, 1)
                sp.dma_start(raw[0:FULL - full, EB - 1, :],
                             a[full * P:FULL * P].rearrange("(p e) -> p e", e=P)).then_inc(came, 16)
                sp.dma_start(raw[FULL - full:FULL - full + 1, EB - 1, 0:TAIL],
                             a[FULL * P:E].rearrange("(p e) -> p e", p=1)).then_inc(came, 16)

            def load_x(i, q, wait):
                if wait:
                    sp.wait_ge(m_h, 2 * i + q - 1)
                sp.dma_start(xb[:, q, :, :], x[ds((2 * i + q) * BATCH * P, BATCH * P), :]
                             .rearrange("(t p) d -> p t d", p=P)).then_inc(x_in[q], 16)

            def store_batch(i, q):
                b = 2 * i + q
                sp.wait_ge(m_relu, b + 1)
                sp.dma_start(table[ds(b * BATCH * P, BATCH * P), :].rearrange("(t p) d -> p t d", p=P),
                             rb[:, q, :, :]).then_inc(r_out[q], 16)

            load_edges(src, src_raw, src_pad, src_in)
            load_x(0, 0, False)
            for k, m in enumerate(weights):
                sp.dma_start(w_nat[:, k, :], m).then_inc(w_in, 16)
            load_x(0, 1, False)
            load_edges(dst, dst_raw, dst_pad, dst_in)
            for k, v in enumerate(vectors):
                sp.dma_start(vec[:, k:k + 1], v.rearrange("(p o) -> p o", o=1)).then_inc(vec_in, 16)
            with sp.Fori(0, NB // 2 - 2) as i:
                for q in range(2):
                    load_x(i + 1, q, True)
                    store_batch(i, q)
            i = NB // 2 - 2
            load_x(i + 1, 0, True)
            store_batch(i, 0)
            sp.wait_ge(m_h, NB - 2)
            first = (NB - 1) * BATCH * P
            sp.dma_start(xb[:, 1, 0:BATCH - 1, :], x[first:(NT - 1) * P, :]
                         .rearrange("(t p) d -> p t d", p=P)).then_inc(x_in[1], 16)
            sp.dma_start(xb[0:LAST, 1, BATCH - 1, :], x[(NT - 1) * P:N, :]).then_inc(x_in[1], 16)
            store_batch(i, 1)
            store_batch(i + 1, 0)
            store_batch(i + 1, 1)
            def load_tile(t, q, last=False):
                rows = LAST if last else P
                sp.dma_start(xn[0:rows, q, :], x[ds(t * P, rows), :]).then_inc(xn_in[q], 16)

            def store_tile(t, q, last=False):
                rows = LAST if last else P
                sp.wait_ge(u_res, t + 1)
                sp.dma_start(out[ds(t * P, rows), :], res[0:rows, q, :]).then_inc(res_out[q], 16)

            sp.wait_ge(flag_set, 1)
            flag = sp.value_load(flag_i[0:1, 0:1], min_val=0, max_val=1)
            with sp.If(flag != 0):
                sp.dma_start(drow[:, :], dst[0:P].rearrange("(o e) -> o e", o=1)).then_inc(g_row, 16)
                with sp.Fori(1, FULL) as j:
                    sp.wait_ge(g_sum, j)
                    sp.dma_start(drow[:, :], dst[ds(j * P, P)].rearrange("(o e) -> o e", o=1)).then_inc(g_row, 16)
                sp.wait_ge(g_sum, FULL)
                sp.dma_start(drow[:, 0:TAIL], dst[FULL * P:E].rearrange("(o e) -> o e", o=1)).then_inc(g_row, 16)

            load_tile(0, 0)
            load_tile(1, 1)
            with sp.Fori(0, NT // 2 - 2) as i:
                for q in range(2):
                    store_tile(2 * i + q, q)
                    sp.wait_ge(res_out[q], 16 * (i + 1))
                    load_tile(2 * i + q + 2, q)
            for t in range(NT - 4, NT):
                store_tile(t, t % 2, last=t == NT - 1)
                if t + 2 < NT:
                    sp.wait_ge(res_out[t % 2], 16 * (t // 2 + 1))
                    load_tile(t + 2, t % 2, last=t + 2 == NT - 1)
            for q in range(2):
                sp.wait_ge(res_out[q], 16 * (NT // 2))

        @block.gpsimd
        def _(pool):
            nc.gpsimd.memset(src_raw[:, EB - 1, :], 0).then_inc(src_pad, 1)
            nc.gpsimd.memset(ident[:, :], 0.0).then_inc(ident_zero, 1)
            pool.wait_ge(ident_zero, 1)
            nc.gpsimd.affine_select(out=ident[:, :], in_=ident[:, :], compare_op=ALU.not_equal, fill=1.0, base=0,
                                    pattern=[[-1, P]], channel_multiplier=1).then_inc(consts, 1)
            nc.gpsimd.iota(win[:, :], pattern=[[1, WIN]], base=0, channel_multiplier=0,
                           allow_small_or_imprecise_dtypes=True).then_inc(consts, 1)
            nc.gpsimd.iota(least[:, :], pattern=[[P, NG]], base=-P, channel_multiplier=0,
                           allow_small_or_imprecise_dtypes=True).then_inc(consts, 1)

            pool.wait_ge(first_in, 16)
            for r in range(NR):
                if r == NR0:
                    pool.wait_ge(idx_set, 1)
                index = idx_first[:, r:r + 1] if r < NR0 else idx[:, r * TPG + RAW:r * TPG + RAW + 1]
                nc.gpsimd.indirect_dma_start(
                    out=x_src[:, r, :], out_offset=None, in_=x,
                    in_offset=bass.IndirectOffsetOnAxis(ap=index, axis=0)).then_inc(x_src_in, 16)
            pool.wait_ge(flag_set, 1)
            for q in range(2):
                pool.wait_ge(r_out[q], 16 * (NB // 2))
            flag = pool.value_load(flag_i[0:1, 0:1], min_val=0, max_val=1)

            def gather(q, k, index):
                return nc.gpsimd.indirect_dma_start(
                    out=gat[:, q, k, :], out_offset=None, in_=table,
                    in_offset=bass.IndirectOffsetOnAxis(ap=index, axis=0))

            def gather_group(i, q, first, tiles=RAW):
                pool.wait_ge(idx_ready, 2 * i + q + 1)
                if not first:
                    pool.wait_ge(group_used, 2 * i + q - 1)
                pool.sem_inc(gathers_begun, 1)
                for k in range(tiles):
                    gather(q, k, idx_now[:, q, k:k + 1]).then_inc(got[q][k], 16)

            with pool.If(flag == 0):
                for q in range(2):
                    gather_group(0, q, True)
                with pool.Fori(1, NG // 2 - 1) as i:
                    for q in range(2):
                        gather_group(i, q, False)
                gather_group(NG // 2 - 1, 0, False)
                gather_group(NG // 2 - 1, 1, False, LASTK)
            with pool.Else():
                def gather_tile(j, first):
                    pool.wait_ge(g_idx, j + 1)
                    if not first:
                        pool.wait_ge(g_turned, j)
                    pool.sem_inc(gathers_begun, 1)
                    gather(0, 0, idx_now[:, 0, 0:1]).then_inc(g_got, 16)

                gather_tile(0, True)
                with pool.Fori(1, ET) as j:
                    gather_tile(j, False)

        @block.tensor
        def _(pe):
            pe.wait_ge(consts, 5)
            pe.wait_ge(src_cast, 1)

            def turn_edges(f, turned):
                for b in range(EB):
                    last = nc.tensor.transpose(flat[:, b * P:(b + 1) * P], f[:, b, :], ident[:, :])
                last.then_inc(turned, 1)

            turn_edges(src_f, src_turned)
            pe.wait_ge(w_in, 16 * len(weights))
            for k in range(len(weights)):
                last = nc.tensor.transpose(flat[:, 2048 + k * P:2048 + (k + 1) * P], w_nat[:, k, :], ident[:, :])
            last.then_inc(w_turned, 1)
            pe.wait_ge(idx_set, 1)
            pe.wait_ge(w_set, 1)

            def turn_h(i, q):
                b = 2 * i + q
                pe.wait_ge(m_h, b + 1)
                if not (isinstance(i, int) and b < 2):
                    pe.wait_ge(m_hTs, b - 1)
                for k in range(BATCH):
                    last = nc.tensor.transpose(psT[q][:, k * P:(k + 1) * P], hb[:, q, k, :], ident[:, :])
                last.then_inc(m_hT, 1)

            def multiply_h(i, q):
                b = 2 * i + q
                pe.wait_ge(m_hTs, b + 1)
                if not (isinstance(i, int) and b < 2):
                    pe.wait_ge(m_relu, b - 1)
                for k in range(BATCH):
                    last = nc.tensor.matmul(psR[q][:, k * P:(k + 1) * P], hTb[:, q, k * P:(k + 1) * P], W1aT,
                                            start=True, stop=True)
                last.then_inc(m_r, 1)

            for q in range(2):
                turn_h(0, q)
                multiply_h(0, q)
            with pe.Fori(1, NB // 2) as i:
                for q in range(2):
                    turn_h(i, q)
                    multiply_h(i, q)
            pe.wait_ge(m_relu, NB)
            pe.wait_ge(dst_cast, 1)
            turn_edges(dst_f, dst_turned)
            pe.wait_ge(dst_set, 1)
            for c, (first, _) in enumerate(CHUNKS):
                last = nc.tensor.matmul(ps[:, 6, c * NG:(c + 1) * NG], ones[0:1, :],
                                        key[0:1, first:NG * TPG:TPG], start=True, stop=True)
            last.then_inc(base_sent, 1)
            pe.wait_ge(bad_set, 1)
            nc.tensor.matmul(ps[0:1, 7, 0:1], ones[:, 0:1], bad[:, 3:4], start=True, stop=True).then_inc(bad_summed, 1)
            pe.wait_ge(diag_set, 2)
            pe.wait_ge(flag_set, 1)

            def sums(t, q):
                pe.wait_ge(u_sums, 2 * t + 2)
                nc.tensor.matmul(pSum[q], sum_now[:, q, :], W1bT, start=True, stop=True)
                nc.tensor.matmul(pCnt[q], cnt_now[:, q, :], ones[0:1, 0:1], start=True, stop=True).then_inc(u_raw, 1)

            def turn_node_h(t, q):
                pe.wait_ge(u_h, t + 1)
                nc.tensor.transpose(pH[q], hn[:, q, :], ident[:, :]).then_inc(u_hT, 1)

            def turn_agg(t, q):
                pe.wait_ge(u_z1, t + 1)
                pe.wait_ge(u_hTs, t + 1)
                nc.tensor.transpose(pZ1[q], z1[:, q, :], ident[:, :]).then_inc(u_z1T, 1)

            def mix(t, q):
                pe.wait_ge(u_hTs, t + 1)
                pe.wait_ge(u_aT, t + 1)
                nc.tensor.matmul(pY[q], hT[:, q, :], diag_h[:, :], start=True, stop=False)
                nc.tensor.matmul(pY[q], aT[:, q, :], diag_a[:, :], start=False, stop=True).then_inc(u_y, 1)

            def turn_fx(t, q):
                pe.wait_ge(u_z2, t + 1)
                nc.tensor.transpose(pZ2[q], z2[:, q, :], ident[:, :]).then_inc(u_z2T, 1)

            def hidden(t, q):
                pe.wait_ge(u_fT, t + 1)
                nc.tensor.matmul(pHid[q], W2fT, fT[:, q, :], start=True, stop=False)
                nc.tensor.matmul(pHid[q], W2gT, aT[:, q, :], start=False, stop=True).then_inc(u_hid, 1)

            def project(t, q):
                pe.wait_ge(u_hids, t + 1)
                nc.tensor.matmul(pOut[q], hid[:, q, :], W2bT, start=True, stop=True).then_inc(u_o, 1)

            steps = {0: sums, 1: turn_node_h, 3: turn_agg, 6: mix, 9: turn_fx, 11: hidden, 14: project}

            def turn_raw(g):
                pe.wait_ge(e_hs, g + 1)
                nc.tensor.transpose(pEh, e_h[:, :], ident[:, :]).then_inc(e_turned, 1)

            def multiply_raw(g):
                pe.wait_ge(e_copied, g + 1)
                nc.tensor.matmul(pEr, e_hT[:, :], W1aT, start=True, stop=True).then_inc(e_made, 1)

            raw_steps = {12: turn_raw, 15: multiply_raw}

            def group(i, q, first=False, nodes=1, tiles=TPG):
                g = 2 * i + q
                pe.wait_ge(hot_ready, g + 1)
                if not first:
                    pe.wait_ge(sums_done, NC * (g - 1))
                    pe.wait_ge(cnts_done, NC * (g - 1))
                for c, (k0, n) in enumerate(CHUNKS):
                    for k in range(k0, min(k0 + n, tiles)):
                        if k == RAW:
                            pe.wait_ge(e_msg, g + 1)
                        else:
                            pe.wait_ge(got[q][k], 16 * (i + 1))
                        nc.tensor.matmul(psS[q][:, c * WIN:(c + 1) * WIN], gat[:, q, k, :], hot[:, q, k, :],
                                         start=k == k0, stop=k == k0 + n - 1)
                        if k == tiles - 1:
                            nc.tensor.matmul(psC[q], ones[:, 0:1], hot_sum[:, q, :, :].rearrange("p c w -> p (c w)"),
                                             start=True, stop=True).then_inc(group_used, 1)
                        if nodes and k in steps:
                            steps[k](g - 3, 1 - q)
                        if tiles == TPG and k in raw_steps and not (isinstance(g, int) and g + 1 == NR):
                            raw_steps[k](g + 1)
                if tiles < TPG:
                    for k in steps:
                        if k >= tiles:
                            steps[k](g - 3, 1 - q)

            flag = pe.value_load(flag_i[0:1, 0:1], min_val=0, max_val=1)
            with pe.If(flag == 0):
                turn_raw(0)
                multiply_raw(0)
                group(0, 0, first=True, nodes=0)
                group(0, 1, first=True, nodes=0)
                group(1, 0, nodes=0)
                group(1, 1)
                with pe.Fori(2, NG // 2 - 1) as i:
                    for q in range(2):
                        group(i, q)
                group(NG // 2 - 1, 0)
                group(NG // 2 - 1, 1, tiles=LASTK)
                for f in steps.values():
                    f(NT - 3, 1)
                for f in (turn_node_h, sums, turn_agg, mix, turn_fx, hidden, project):
                    for q in range(2):
                        f(NT - 2 + q, q)
            with pe.Else():
                def turn_tile(j, first):
                    pe.wait_ge(g_got, 16 * (j + 1))
                    if not first:
                        pe.wait_ge(g_copied, j)
                    nc.tensor.transpose(ps[:, 0, 0:P], gat[:, 0, 0, :], ident[:, :]).then_inc(g_turned, 1)

                turn_tile(0, True)
                with pe.Fori(1, ET) as j:
                    turn_tile(j, False)
                with pe.Fori(0, NT // 2) as i:
                    for q in range(2):
                        for k in steps:
                            steps[k](2 * i + q, q)

        @block.scalar
        def _(act):
            act.wait_ge(consts, 5)

            def std(i, q):
                b = 2 * i + q
                act.wait_ge(m_var, b + 1)
                nc.scalar.activation(sd1[:, q, :], var1[:, q, :], ACT.Sqrt, bias=eps[:, 0:1]).then_inc(m_std, 1)

            def normalise(i, q):
                b = 2 * i + q
                act.wait_ge(m_norm, b + 1)
                if not (isinstance(i, int) and b < 2):
                    act.wait_ge(m_hT, b - 1)
                for k in range(BATCH):
                    last = nc.scalar.activation(hb[:, q, k, :], xb[:, q, k, :], ACT.Relu,
                                                scale=rs1[:, q, k:k + 1], bias=nm1[:, q, k:k + 1])
                last.then_inc(m_h, 1)

            def relu(i, q):
                b = 2 * i + q
                act.wait_ge(m_r, b + 1)
                if not (isinstance(i, int) and b < 2):
                    act.wait_ge(r_out[q], 16 * i)
                nc.scalar.activation(rb[:, q, :, :].rearrange("p t d -> p (t d)"), psR[q], ACT.Relu).then_inc(m_relu, 1)

            std(0, 0)
            normalise(0, 0)
            std(0, 1)
            normalise(0, 1)
            relu(0, 0)
            std(1, 0)
            normalise(1, 0)
            relu(0, 1)
            with act.Fori(1, NB // 2 - 1) as i:
                std(i, 1)
                normalise(i, 1)
                relu(i, 0)
                std(i + 1, 0)
                normalise(i + 1, 0)
                relu(i, 1)
            i = NB // 2 - 1
            std(i, 1)
            normalise(i, 1)
            relu(i, 0)
            relu(i, 1)

            def node_h(t, q, i):
                act.wait_ge(xn_in[q], 16 * (i + 1))
                nc.scalar.activation(hn[:, q, :], xn[:, q, :], ACT.Relu, scale=rs_all[:, ds(t, 1)],
                                     bias=nm_all[:, ds(t, 1)]).then_inc(u_h, 1)

            def keep_node_h(t, q, i):
                act.wait_ge(u_hT, t + 1)
                nc.scalar.copy(hT[:, q, :], pH[q]).then_inc(u_hTs, 1)

            def std_sum(t, q, i):
                act.wait_ge(u_small, 3 * t + 3)
                nc.scalar.activation(small[:, q, 3:4], small[:, q, 2:3], ACT.Sqrt).then_inc(u_std, 1)

            def scale_agg(t, q, i):
                act.wait_ge(u_z1T, t + 1)
                nc.scalar.activation(aT[:, q, :], pZ1[q], ACT.Identity, scale=vec[:, 0:1],
                                     bias=vec[:, 1:2]).then_inc(u_aT, 1)

            def std_mix(t, q, i):
                act.wait_ge(u_var2, t + 1)
                nc.scalar.activation(small[:, q, 5:6], mv3[:, q, 1:2], ACT.Sqrt, bias=eps[:, 0:1]).then_inc(u_std2, 1)

            def scale_fx(t, q, i):
                act.wait_ge(u_z2T, t + 1)
                nc.scalar.activation(fT[:, q, :], pZ2[q], ACT.Identity, scale=vec[:, 3:4],
                                     bias=vec[:, 4:5]).then_inc(u_fT, 1)

            def relu_hidden(t, q, i):
                act.wait_ge(u_hid, t + 1)
                nc.scalar.activation(hid[:, q, :], pHid[q], ACT.Relu).then_inc(u_hids, 1)

            def raw_std(g):
                act.wait_ge(e_var, g + 1)
                nc.scalar.activation(e_sc[:, 0:1], e_mv[:, 1:2], ACT.Sqrt, bias=eps[:, 0:1]).then_inc(e_std, 1)

            def raw_h(g):
                act.wait_ge(e_norm, g + 1)
                nc.scalar.activation(e_h[:, :], x_src[:, ds(g, 1), :].rearrange("p o d -> p (o d)"), ACT.Relu,
                                     scale=e_sc[:, 1:2], bias=e_sc[:, 2:3]).then_inc(e_hs, 1)

            def raw_keep(g):
                act.wait_ge(e_turned, g + 1)
                nc.scalar.copy(e_hT[:, :], pEh).then_inc(e_copied, 1)

            def raw_relu(g, q, first):
                act.wait_ge(e_made, g + 1)
                if not first:
                    act.wait_ge(group_used, g - 1)
                nc.scalar.activation(gat[:, q, RAW, :], pEr, ACT.Relu).then_inc(e_msg, 1)

            update = (node_h, std_sum, keep_node_h, scale_agg, std_mix, scale_fx, relu_hidden)

            def group(i, q, nodes=1, raws=1):
                g = 2 * i + q
                node = (g - 3, 1 - q, i - 2 + q)
                if nodes:
                    for f in update:
                        f(*node)
                if raws:
                    raw_std(g + 1)
                    raw_h(g + 1)
                    raw_keep(g + 1)
                    raw_relu(g + 1, 1 - q, False)

            act.wait_ge(vec_in, 16 * len(vectors))
            act.wait_ge(flag_set, 1)
            flag = act.value_load(flag_i[0:1, 0:1], min_val=0, max_val=1)
            with act.If(flag == 0):
                raw_std(0)
                raw_h(0)
                raw_keep(0)
                raw_relu(0, 0, True)
                raw_std(1)
                raw_h(1)
                raw_keep(1)
                raw_relu(1, 1, True)
                group(0, 1, nodes=0)
                group(1, 0, nodes=0)
                group(1, 1)
                with act.Fori(2, NG // 2 - 1) as i:
                    for q in range(2):
                        group(i, q)
                for q in range(2):
                    group(NG // 2 - 1, q, raws=0)
                for f in update:
                    f(NT - 3, 1, NT // 2 - 2)
                for f in update:
                    for q in range(2):
                        f(NT - 2 + q, q, NT // 2 - 1)
            with act.Else():
                with act.Fori(0, NT // 2) as i:
                    for q in range(2):
                        for f in update:
                            f(2 * i + q, q, i)

        @block.vector
        def _(dve):
            nc.vector.memset(ones[:, :], 1.0).then_inc(consts, 1)
            nc.vector.memset(eps[:, :], EPS).then_inc(consts, 1)
            nc.vector.memset(dst_raw[:, EB - 1, :], N).then_inc(dst_pad, 1)
            nc.vector.memset(idx[:, EB * P:], 0)
            nc.vector.memset(key[:, EB * P:NG * TPG], float(N))
            nc.vector.memset(key[:, NG * TPG:], 0.0)
            dve.wait_ge(src_in, 48)
            nc.vector.tensor_copy(src_f[:, :, :], src_raw[:, :, :]).then_inc(src_cast, 1)
            dve.wait_ge(src_turned, 1)
            nc.vector.tensor_copy(idx[:, 0:EB * P], flat[:, 0:EB * P]).then_inc(idx_set, 1)
            dve.wait_ge(w_turned, 1)
            nc.vector.tensor_copy(w_T[:, :, :].rearrange("p k d -> p (k d)"),
                                  flat[:, 2048:2048 + 5 * P]).then_inc(w_set, 1)

            def find_keys():
                dve.wait_ge(dst_turned, 1)
                nc.vector.tensor_copy(key[:, 0:EB * P], flat[:, 0:EB * P]).then_inc(dst_set, 1)
                dve.wait_ge(base_sent, 1)
                nc.vector.tensor_copy(base_b[:, :, :].rearrange("p g c -> p c g"),
                                      ps[:, 6, 0:NC * NG].rearrange("p (c g) -> p c g", c=NC)).then_inc(prep, 1)
                dve.wait_ge(prep, 1)
                dve.wait_ge(dst_set, 1)
                nc.vector.tensor_copy(base_i[:, :], base_b[0:1, :, :].rearrange("p g c -> p (g c)")).then_inc(prep, 1)
                by_group = key[:, 0:NG * TPG].rearrange("p (g k) -> p g k", k=TPG)
                for c, (k0, n) in enumerate(CHUNKS):
                    nc.vector.tensor_tensor(by_group[:, :, k0:k0 + n], by_group[:, :, k0:k0 + n],
                                            base_b[:, :, c:c + 1].broadcast_to([P, NG, n]), ALU.subtract).then_inc(prep, 1)
                nc.vector.tensor_tensor(slack[:, :, :], base_b[:, :, :],
                                        least[:, :].unsqueeze(2).broadcast_to([P, NG, NC]), ALU.subtract).then_inc(prep, 1)
                dve.wait_ge(prep, 6)
                nc.vector.tensor_reduce(bad[:, 0:1], key[:, 0:NG * TPG], AX.X, ALU.max).then_inc(prep, 1)
                nc.vector.tensor_reduce(bad[:, 1:2], key[:, 0:NG * TPG], AX.X, ALU.min).then_inc(prep, 1)
                nc.vector.tensor_reduce(bad[:, 2:3], slack[:, :, :], AX.XY, ALU.min).then_inc(prep, 1)
                dve.wait_ge(prep, 9)
                nc.vector.tensor_scalar(bad[:, 3:4], bad[:, 0:1], float(WIN), None, ALU.is_ge).then_inc(prep, 1)
                for m in (1, 2):
                    dve.wait_ge(prep, 9 + m)
                    last = nc.vector.scalar_tensor_tensor(out=bad[:, 3:4], in0=bad[:, m:m + 1], scalar=0.0,
                                                          in1=bad[:, 3:4], op0=ALU.is_lt, op1=ALU.add)
                    last.then_inc(prep if m == 1 else bad_set, 1)
                dve.wait_ge(bad_summed, 1)
                nc.vector.tensor_scalar(flag_i[:, :], ps[0:1, 7, 0:1], 1.0, None, ALU.min).then_inc(flag_set, 1)

            def set_diagonals():
                dve.wait_ge(vec_in, 16 * len(vectors))
                dve.wait_ge(consts, 5)
                nc.vector.tensor_scalar(vec2[:, 0:1], vec[:, 2:3], 1.0, None, ALU.add).then_inc(vec_set, 1)
                nc.vector.tensor_scalar(vec2[:, 1:2], vec[:, 2:3], -1.0, None, ALU.mult).then_inc(vec_set, 1)
                dve.wait_ge(vec_set, 2)
                nc.vector.tensor_scalar(diag_h[:, :], ident[:, :], vec2[:, 0:1], None, ALU.mult).then_inc(diag_set, 1)
                nc.vector.tensor_scalar(diag_a[:, :], ident[:, :], vec2[:, 1:2], None, ALU.mult).then_inc(diag_set, 1)

            def stats(i, q, extra=0):
                b = 2 * i + q
                dve.wait_ge(x_in[q], 16 * (i + 1) + extra)
                for k in range(BATCH):
                    last = nc.vector.bn_stats(st1[:, q, k, :], xb[:, q, k, :])
                last.then_inc(m_stats, 1)
                dve.wait_ge(m_stats, b + 1)
                ev, od = st1[:, q, :, 0:3], st1[:, q, :, 3:6]
                nc.vector.tensor_tensor(mean2[:, q, :], ev[:, :, 1], od[:, :, 1], ALU.add)
                nc.vector.tensor_tensor(apart[:, q, :], ev[:, :, 1], od[:, :, 1], ALU.subtract)
                nc.vector.tensor_tensor(spread[:, q, :], ev[:, :, 2], od[:, :, 2], ALU.add).then_inc(m_joined, 1)
                dve.wait_ge(m_joined, 2 * b + 1)
                nc.vector.scalar_tensor_tensor(out=apart2[:, q, :], in0=apart[:, q, :], scalar=0.25, in1=apart[:, q, :],
                                               op0=ALU.mult, op1=ALU.mult).then_inc(m_joined, 1)
                dve.wait_ge(m_joined, 2 * b + 2)
                nc.vector.scalar_tensor_tensor(out=var1[:, q, :], in0=spread[:, q, :], scalar=1.0 / D, in1=apart2[:, q, :],
                                               op0=ALU.mult, op1=ALU.add).then_inc(m_var, 1)
                dve.wait_ge(m_std, b + 1)
                if not (isinstance(i, int) and b < 2):
                    dve.wait_ge(m_h, b - 1)
                nc.vector.reciprocal(rs1[:, q, :], sd1[:, q, :]).then_inc(m_rstd, 1)
                nc.vector.reciprocal(rs_all[:, ds(b * BATCH, BATCH)], sd1[:, q, :])
                dve.wait_ge(m_rstd, b + 1)
                nc.vector.scalar_tensor_tensor(out=nm1[:, q, :], in0=mean2[:, q, :], scalar=-0.5, in1=rs1[:, q, :],
                                               op0=ALU.mult, op1=ALU.mult).then_inc(m_norm, 1)
                nc.vector.scalar_tensor_tensor(out=nm_all[:, ds(b * BATCH, BATCH)], in0=mean2[:, q, :], scalar=-0.5,
                                               in1=rs1[:, q, :], op0=ALU.mult, op1=ALU.mult)

            def keep_h(i, q):
                b = 2 * i + q
                dve.wait_ge(m_hT, b + 1)
                if not (isinstance(i, int) and b < 2):
                    dve.wait_ge(m_r, b - 1)
                nc.vector.tensor_copy(hTb[:, q, :], psT[q]).then_inc(m_hTs, 1)

            stats(0, 0)
            stats(0, 1)
            keep_h(0, 0)
            stats(1, 0)
            keep_h(0, 1)
            with dve.Fori(1, NB // 2 - 1) as i:
                stats(i, 1)
                keep_h(i, 0)
                stats(i + 1, 0)
                keep_h(i, 1)
            i = NB // 2 - 1
            stats(i, 1, extra=16)
            keep_h(i, 0)
            keep_h(i, 1)
            dve.wait_ge(dst_in, 48)
            nc.vector.tensor_copy(dst_f[:, :, :], dst_raw[:, :, :]).then_inc(dst_cast, 1)
            set_diagonals()
            find_keys()

            def ready_indices(i, q, first=False):
                g = 2 * i + q
                if not first:
                    dve.wait_ge(group_used, g - 1)
                nc.vector.tensor_copy(idx_now[:, q, :], idx[:, ds(g * TPG, TPG)]).then_inc(idx_ready, 1)

            def ready_hot(i, q):
                g = 2 * i + q
                nc.vector.tensor_tensor(hot[:, q, :, :], win[:, :].unsqueeze(1).broadcast_to([P, TPG, WIN]),
                                        key[:, ds(g * TPG, TPG)].unsqueeze(2).broadcast_to([P, TPG, WIN]),
                                        ALU.is_equal).then_inc(hot_made, 1)

            def ready_counts(i, q):
                dve.wait_ge(hot_made, 2 * i + q + 1)
                for c, (k0, n) in enumerate(CHUNKS):
                    last = nc.vector.tensor_reduce(hot_sum[:, q, c, :], hot[:, q, k0:k0 + n, :].rearrange("p k w -> p w k"),
                                                   AX.X, ALU.add)
                last.then_inc(hot_ready, 1)

            def ready_group(i, q, first):
                ready_indices(i, q, first)
                ready_hot(i, q)
                ready_counts(i, q)

            def load_bases(i, q, chunks=NC):
                return [dve.value_load(base_i[0:1, ds((2 * i + q) * NC + c, 1)], min_val=0, max_val=N)
                        for c in range(chunks)]

            def add_group(i, q, bases):
                g = 2 * i + q
                dve.wait_ge(group_used, g + 1)
                for c, at in enumerate(bases):
                    dve.wait_ge(sums_done, g * NC + c)
                    nc.vector.tensor_tensor(acc[:, ds(at, WIN)], acc[:, ds(at, WIN)],
                                            psS[q][:, c * WIN:(c + 1) * WIN], ALU.add).then_inc(sums_done, 1)
                    dve.wait_ge(cnts_done, g * NC + c)
                    nc.vector.tensor_tensor(cnt[:, ds(at, WIN)], cnt[:, ds(at, WIN)],
                                            psC[q][:, c * WIN:(c + 1) * WIN], ALU.add).then_inc(cnts_done, 1)

            def raw_stats(g):
                nc.vector.bn_stats(e_st[:, :], x_src[:, ds(g, 1), :].rearrange("p o d -> p (o d)"))
                dve.drain()
                nc.vector.bn_aggr(e_mv[:, :], e_st[:, :]).then_inc(e_var, 1)
                dve.wait_ge(e_std, g + 1)
                nc.vector.reciprocal(e_sc[:, 1:2], e_sc[:, 0:1]).then_inc(e_rstd, 1)
                dve.wait_ge(e_var, g + 1)
                dve.wait_ge(e_rstd, g + 1)
                nc.vector.scalar_tensor_tensor(out=e_sc[:, 2:3], in0=e_mv[:, 0:1], scalar=-1.0, in1=e_sc[:, 1:2],
                                               op0=ALU.mult, op1=ALU.mult).then_inc(e_norm, 1)

            def take_sums(t, q, i):
                nc.vector.tensor_copy(sum_now[:, q, :], acc[:, ds(t * P, P)]).then_inc(u_sums, 1)
                nc.vector.tensor_copy(cnt_now[:, q, :], cnt[:, ds(t * P, P)]).then_inc(u_sums, 1)

            def agg_stats(t, q, i):
                dve.wait_ge(u_raw, t + 1)
                nc.vector.bn_stats(st2[:, q, :], pSum[q])
                nc.vector.tensor_scalar(small[:, q, 0:1], pCnt[q], 1.0, None, ALU.max).then_inc(u_small, 1)
                dve.wait_ge(u_small, 3 * t + 1)
                nc.vector.scalar_tensor_tensor(out=small[:, q, 1:2], in0=small[:, q, 0:1], scalar=EPS,
                                               in1=small[:, q, 0:1], op0=ALU.mult, op1=ALU.mult).then_inc(u_small, 1)
                dve.drain()
                nc.vector.bn_aggr(mv2[:, q, :], st2[:, q, :]).then_inc(u_var, 1)
                dve.wait_ge(u_small, 3 * t + 2)
                dve.wait_ge(u_var, t + 1)
                nc.vector.tensor_tensor(small[:, q, 2:3], small[:, q, 1:2], mv2[:, q, 1:2], ALU.add).then_inc(u_small, 1)

            def agg_norm(t, q, i):
                dve.wait_ge(u_std, t + 1)
                nc.vector.reciprocal(small[:, q, 4:5], small[:, q, 3:4]).then_inc(u_scale, 1)
                dve.wait_ge(u_scale, t + 1)
                nc.vector.tensor_scalar(z1[:, q, :], pSum[q], mv2[:, q, 0:1], small[:, q, 4:5],
                                        ALU.subtract, ALU.mult).then_inc(u_z1, 1)

            def mix_stats(t, q, i):
                dve.wait_ge(u_y, t + 1)
                nc.vector.bn_stats(st3[:, q, :], pY[q])
                dve.drain()
                nc.vector.bn_aggr(mv3[:, q, :], st3[:, q, :]).then_inc(u_var2, 1)

            def mix_norm(t, q, i):
                dve.wait_ge(u_std2, t + 1)
                nc.vector.reciprocal(small[:, q, 6:7], small[:, q, 5:6]).then_inc(u_scale2, 1)
                dve.wait_ge(u_scale2, t + 1)
                dve.wait_ge(u_var2, t + 1)
                nc.vector.tensor_scalar(z2[:, q, :], pY[q], mv3[:, q, 0:1], small[:, q, 6:7],
                                        ALU.subtract, ALU.mult).then_inc(u_z2, 1)

            def residual(t, q, i):
                dve.wait_ge(u_o, t + 1)
                dve.wait_ge(xn_in[q], 16 * (i + 1))
                nc.vector.tensor_tensor(res[:, q, :], pOut[q], xn[:, q, :], ALU.add).then_inc(u_res, 1)

            update = (take_sums, agg_stats, agg_norm, mix_stats, mix_norm, residual)
            dve.wait_ge(flag_set, 1)
            flag = dve.value_load(flag_i[0:1, 0:1], min_val=0, max_val=1)

            def clear():
                nc.vector.memset(acc[:, :], 0.0).then_inc(acc_zero, 1)
                for q in range(2):
                    dve.wait_ge(r_out[q], 16 * (NB // 2))
                nc.vector.memset(cnt[:, :], 0.0).then_inc(acc_zero, 1)

            with dve.If(flag == 0):
                dve.wait_ge(x_src_in, 16 * NR)
                ready_group(0, 0, True)
                raw_stats(0)
                ready_group(0, 1, True)
                raw_stats(1)
                clear()
                dve.wait_ge(acc_zero, 2)
                add_group(0, 0, load_bases(0, 0))
                ready_group(1, 0, False)
                raw_stats(2)
                add_group(0, 1, load_bases(0, 1))
                ready_group(1, 1, False)
                raw_stats(3)
                dve.wait_ge(sums_done, NC * 2)
                dve.wait_ge(cnts_done, NC * 2)
                take_sums(0, 0, 0)

                def body(i, q, last=False):
                    g = 2 * i + q
                    node = (g - 3, 1 - q, i - 2 + q)
                    bases = load_bases(i - 1 + q, 1 - q)
                    if not last:
                        ready_indices(i + q, 1 - q)
                    agg_stats(*node)
                    agg_norm(*node)
                    if not last:
                        ready_hot(i + q, 1 - q)
                    mix_stats(*node)
                    mix_norm(*node)
                    if not (isinstance(g, int) and g + 1 >= NR):
                        raw_stats(g + 1)
                    add_group(i - 1 + q, 1 - q, bases)
                    if not last:
                        ready_counts(i + q, 1 - q)
                    residual(*node)
                    dve.wait_ge(sums_done, NC * g)
                    dve.wait_ge(cnts_done, NC * g)
                    take_sums(g - 2, q, i - 1)

                body(1, 1)
                with dve.Fori(2, NG // 2 - 1) as i:
                    for q in range(2):
                        body(i, q)
                body(NG // 2 - 1, 0)
                body(NG // 2 - 1, 1, last=True)
                for f in update[1:]:
                    f(NT - 3, 1, NT // 2 - 2)
                chunks = sum(k0 < LASTK for k0, _ in CHUNKS)
                add_group(NG // 2 - 1, 1, load_bases(NG // 2 - 1, 1, chunks))
                last = NC * (NG - 1) + chunks
                dve.wait_ge(sums_done, last)
                dve.wait_ge(cnts_done, last)
                for f in update:
                    for q in range(2):
                        f(NT - 2 + q, q, NT // 2 - 1)
            with dve.Else():
                clear()
                dve.wait_ge(acc_zero, 2)

                def add_edges(j, n):
                    dve.wait_ge(g_row, 16 * (j + 1))
                    dve.wait_ge(g_turned, j + 1)
                    nc.vector.tensor_copy(gT[:, :], ps[:, 0, 0:P]).then_inc(g_copied, 1)
                    dve.drain()
                    with dve.Fori(0, n) as e:
                        at = dve.value_load(drow[0:1, ds(e, 1)], min_val=0, max_val=N - 1)
                        nc.vector.tensor_tensor(acc[:, ds(at, 1)], acc[:, ds(at, 1)], gT[:, ds(e, 1)], ALU.add)
                        nc.vector.tensor_tensor(cnt[:, ds(at, 1)], cnt[:, ds(at, 1)], ones[0:1, 0:1], ALU.add)
                        dve.drain()
                    dve.drain().then_inc(g_sum, 1)

                with dve.Fori(0, FULL) as j:
                    nc.vector.tensor_copy(idx_now[:, 0, 0:1], idx[:, ds(j, 1)]).then_inc(g_idx, 1)
                    add_edges(j, P)
                nc.vector.tensor_copy(idx_now[:, 0, 0:1], idx[:, FULL:FULL + 1]).then_inc(g_idx, 1)
                add_edges(FULL, TAIL)
                dve.wait_ge(g_sum, ET)
                with dve.Fori(0, NT // 2) as i:
                    for q in range(2):
                        for f in update:
                            f(2 * i + q, q, i)


_INS = ['x', 'src', 'dst', 'L0_gnn_W1a', 'L0_gnn_W1b', 'L0_gnn_ln1_g', 'L0_gnn_ln1_b', 'L0_gnn_w', 'L0_gnn_ln2_g',
        'L0_gnn_ln2_b', 'L0_gnn_W2a', 'L0_gnn_W2b']


def kernel(**inputs):
    import numpy as _np
    import concourse.bacc as _bacc
    from concourse import mybir as _mybir
    from concourse.bass_utils import run_bass_kernel_spmd as _run

    nc = _bacc.Bacc("TRN2", target_bir_lowering=False, num_devices=1)
    arrays, args = {}, []
    for name in _INS:
        a = _np.ascontiguousarray(inputs[name])
        arrays[f"in_{name}_dram"] = a
        args.append(nc.dram_tensor(f"in_{name}_dram", a.shape, _mybir.dt.from_np(a.dtype), kind="ExternalInput").ap())
    out = nc.dram_tensor("out_0_dram", inputs['x'].shape, _mybir.dt.float32, kind="ExternalOutput").ap()
    gnn_kernel(nc, *args, out)
    r = _run(nc, [arrays], core_ids=[0])
    return r.results[0]["out_0_dram"]
```

```python
from contextlib import ExitStack

import concourse.bass as bass
from concourse import mybir

F32 = mybir.dt.float32
I32 = mybir.dt.int32
ALU = mybir.AluOpType
ACT = mybir.ActivationFunctionType
AX = mybir.AxisListType
ds = bass.ds

P = 128
EPS = 1e-5
WIN = 64
BATCH = 7
CHUNKS = ((0, 6), (6, 6), (12, 5))


def gnn_kernel(nc, x, src, dst, W1a, W1b, ln1_g, ln1_b, w, ln2_g, ln2_b, W2a, W2b, out):
    N, D = x.shape
    E, = src.shape
    NT = -(-N // P)
    NPAD = NT * P
    LAST = N - (NT - 1) * P
    ET = -(-E // P)
    TPG = sum(n for _, n in CHUNKS)
    NG = -(-ET // TPG)
    NC = len(CHUNKS)
    EB = -(-ET // P)
    NB = NT // BATCH
    FULL = E // P
    TAIL = E - FULL * P
    LASTK = ET - (NG - 1) * TPG
    RAW = TPG - 1
    NR = NG - 1
    NR0 = 9
    ACC = max(NPAD, N + WIN)
    assert D == P and NT % BATCH == 0 and NB % 2 == 0 and NG == NT and NG % 2 == 0
    assert LASTK < TPG and [c for c in CHUNKS if c[0] < LASTK] == [c for c in CHUNKS if sum(c) <= LASTK]
    assert LASTK > 8
    assert CHUNKS[-1][0] + CHUNKS[-1][1] == TPG and N + WIN <= ACC

    table = nc.dram_tensor("messages", [NPAD, D], F32, kind="Internal").ap()

    with ExitStack() as ctx:
        def sb(name, shape, dt=F32):
            return ctx.enter_context(nc.sbuf_tensor(name, shape, dt))

        def sem(name):
            return ctx.enter_context(nc.semaphore(name))

        acc = sb("acc", [P, ACC])
        cnt_rows = sb("cnt_rows", [P, ACC])
        cnt = cnt_rows[0:1, :]
        x_src = sb("x_src", [P, NR, D])
        gat = sb("gat", [P, 2, TPG, D])
        hot = sb("hot", [P, 2, TPG, WIN])
        hot_sum = sb("hot_sum", [P, 2, NC, WIN])
        idx_now = sb("idx_now", [P, 2, TPG], I32)
        idx_first = sb("idx_first", [P, NR0], I32)

        def early(whole, at, *shape):
            size = 1
            for n in shape:
                size *= n
            a = whole[:, at:at + size]
            names = "abc"[:len(shape)]
            return a.rearrange(f"p ({' '.join(names)}) -> p {' '.join(names)}", **dict(zip(names, shape)))

        src_raw = early(acc, 0, EB, P).bitcast(I32)
        dst_raw = early(acc, EB * P, EB, P).bitcast(I32)
        src_f = early(acc, 2 * EB * P, EB, P)
        dst_f = early(acc, 3 * EB * P, EB, P)
        x_all = early(cnt_rows, 0, NT, D)
        gat_flat = gat[:, :, :, :].rearrange("p q k d -> p (q k d)")
        hb = early(gat_flat, 0, 2, BATCH, D)
        hTb = early(gat_flat, 2 * BATCH * D, 2, BATCH * P)
        rb = early(hot[:, :, :, :].rearrange("p q k w -> p (q k w)"), 0, 2, BATCH, D)
        idx = sb("idx", [P, (NG + 1) * TPG], I32)
        key = sb("key", [P, (NG + 1) * TPG])
        base_b = early(acc, 5 * EB * P + 5 * P, NG, NC)
        base_i = sb("base_i", [1, NG * NC], I32)
        least = early(acc, 4 * EB * P, NG)
        slack = early(acc, 4 * EB * P + NG, NG, NC)
        bad = sb("bad", [P, 4])
        flag_i = sb("flag_i", [1, 1], I32)
        ident = sb("ident", [P, P])
        ones = sb("ones", [P, P])
        win = sb("win", [P, WIN])
        eps = sb("eps", [P, 1])
        w_nat = early(acc, 5 * EB * P, 5, P)
        w_T = sb("w_T", [P, 5, P])
        vec = sb("vec", [P, 5])
        vec2 = sb("vec2", [P, 2])
        diag_h = sb("diag_h", [P, P])
        diag_a = sb("diag_a", [P, P])
        st1 = sb("st1", [P, 2, BATCH, 6])
        mean2, apart, spread, apart2, var1, sd1 = (
            sb(n, [P, 2, BATCH]) for n in ("mean2", "apart", "spread", "apart2", "var1", "sd1"))
        rs_all = sb("rs_all", [P, NT])
        nm_all = sb("nm_all", [P, NT])
        e_st = sb("e_st", [P, 6])
        e_mv = sb("e_mv", [P, 2])
        e_sc = sb("e_sc", [P, 3])
        e_h = sb("e_h", [P, D])
        e_hT = sb("e_hT", [P, P])
        xn = sb("xn", [P, 2, D])
        x_last = x_src[:, 0:2, :]
        hn = sb("hn", [P, 2, D])
        hT = sb("hT", [P, 2, P])
        sum_now = sb("sum_now", [P, 2, P])
        cnt_now = sb("cnt_now", [1, 2, P])
        st2 = sb("st2", [P, 2, 6])
        mv2 = sb("mv2", [P, 2, 2])
        small = sb("small", [P, 2, 8])
        z1 = sb("z1", [P, 2, D])
        aT = sb("aT", [P, 2, P])
        st3 = sb("st3", [P, 2, 6])
        mv3 = sb("mv3", [P, 2, 2])
        z2 = sb("z2", [P, 2, D])
        fT = sb("fT", [P, 2, P])
        hid = sb("hid", [P, 2, P])
        res = sb("res", [P, 2, D])

        def late(t):
            return isinstance(t, int) and t >= NT - 2

        def x_of(t, q):
            return x_last[:, q, :] if late(t) else xn[:, q, :]

        drow = e_h[0:1, :].bitcast(I32)
        gT = e_hT

        ps = ctx.enter_context(nc.psum_tensor("ps", [P, 8, 512], F32))
        flat = ps[:, :, :].rearrange("p b c -> p (b c)")
        psT = [flat[:, 0:BATCH * P], flat[:, 1024:1024 + BATCH * P]]
        psR = [flat[:, 2048:2048 + BATCH * P], flat[:, 3072:3072 + BATCH * P]]
        psS = [ps[:, q, 0:NC * WIN] for q in range(2)]
        psC = [ps[0:1, q, 256:256 + NC * WIN] for q in range(2)]
        pEh, pEr = ps[:, 2, 0:P], ps[:, 2, 128:256]
        pWin = ps[:, 7, 512 - WIN:512]
        pSum, pY, pOut = ([ps[:, b, a:a + P] for b in (3, 4, 0, 2)] for a in (0, 128, 256))
        pCnt = [ps[:, b, 384:385] for b in (3, 4, 0, 2)]
        pH, pZ1, pZ2, pHid = ([ps[:, b, a:a + P] for b in (5, 6, 5, 7)] for a in (0, 128, 256, 384))

        def bank(t, q):
            return q + 2 if late(t) else q

        src_pad, dst_pad, x_pad = sem("src_pad"), sem("dst_pad"), sem("x_pad")
        src_in, dst_in = sem("src_in"), sem("dst_in")
        w_in, vec_in = sem("w_in"), sem("vec_in")
        ident_zero, consts = sem("ident_zero"), sem("consts")
        src_cast, dst_cast = sem("src_cast"), sem("dst_cast")
        src_turned, dst_turned = sem("src_turned"), sem("dst_turned")
        idx_set, dst_set = sem("idx_set"), sem("dst_set")
        base_sent = sem("base_sent")
        prep = sem("prep")
        win_set = sem("win_set")
        bad_set, bad_summed, flag_set = sem("bad_set"), sem("bad_summed"), sem("flag_set")
        w_turned, w_set = sem("w_turned"), sem("w_set")
        vec_set, diag_set = sem("vec_set"), sem("diag_set")
        acc_zero = sem("acc_zero")
        x_in = [sem("x_in0"), sem("x_in1")]
        m_stats, m_joined, m_var, m_std, m_rstd, m_norm = (
            sem(n) for n in ("m_stats", "m_joined", "m_var", "m_std", "m_rstd", "m_norm"))
        m_h, m_hT, m_hTs, m_r, m_relu = (sem(n) for n in ("m_h", "m_hT", "m_hTs", "m_r", "m_relu"))
        r_out = [sem("r_out0"), sem("r_out1")]
        idx_ready = sem("idx_ready")
        got = [[sem(f"got{q}_{k}") for k in range(TPG)] for q in range(2)]
        gathers_begun = sem("gathers_begun")
        hot_made = sem("hot_made")
        hot_ready = sem("hot_ready")
        group_used = sem("group_used")
        sums_done, cnts_done = sem("sums_done"), sem("cnts_done")
        xn_in = [sem("xn_in0"), sem("xn_in1")]
        first_in, x_src_in, x_last_in = sem("first_in"), sem("x_src_in"), sem("x_last_in")
        e_var, e_std, e_rstd, e_norm, e_hs, e_turned, e_copied, e_made, e_msg = (
            sem(n) for n in ("e_var", "e_std", "e_rstd", "e_norm", "e_hs", "e_turned", "e_copied", "e_made", "e_msg"))
        u_h, u_hT, u_hTs = sem("u_h"), sem("u_hT"), sem("u_hTs")
        u_sums = sem("u_sums")
        u_raw, u_small, u_var, u_std, u_scale, u_z1, u_z1T, u_aT, u_y = (
            sem(n) for n in ("u_raw", "u_small", "u_var", "u_std", "u_scale", "u_z1", "u_z1T", "u_aT", "u_y"))
        u_var2, u_std2, u_scale2, u_z2, u_z2T, u_fT, u_hid, u_hids, u_o, u_res = (
            sem(n) for n in ("u_var2", "u_std2", "u_scale2", "u_z2", "u_z2T", "u_fT", "u_hid", "u_hids", "u_o", "u_res"))
        res_out = [sem("res_out0"), sem("res_out1")]
        g_idx, g_row, g_got, g_turned, g_copied, g_sum = (
            sem(n) for n in ("g_idx", "g_row", "g_got", "g_turned", "g_copied", "g_sum"))

        vectors = (ln1_g, ln1_b, w, ln2_g, ln2_b)
        weights = (W1a, W1b, W2b, W2a[:, 0:D], W2a[:, D:2 * D])
        W1aT, W1bT, W2bT, W2fT, W2gT = (w_T[:, i, :] for i in range(5))

        block = ctx.enter_context(nc.Block())

        @block.sync
        def _(sp):
            sp.dma_start(idx_first[:, :], src[0:NR0 * TPG * P].rearrange("(g k p) -> p g k", k=TPG, p=P)[:, :, RAW],
                         allow_slow_non_contiguous=True).then_inc(first_in, 16)

            def load_edges(a, raw, pad, came):
                full = (EB - 1) * P
                sp.dma_start(raw[:, 0:EB - 1, :],
                             a[0:full * P].rearrange("(b p e) -> p b e", p=P, e=P)).then_inc(came, 16)
                sp.wait_ge(pad, 1)
                sp.dma_start(raw[0:FULL - full, EB - 1, :],
                             a[full * P:FULL * P].rearrange("(p e) -> p e", e=P)).then_inc(came, 16)
                sp.dma_start(raw[FULL - full:FULL - full + 1, EB - 1, 0:TAIL],
                             a[FULL * P:E].rearrange("(p e) -> p e", p=1)).then_inc(came, 16)

            def load_x(i, q):
                if not (isinstance(i, int) and i == 0):
                    sp.wait_ge(x_in[q], 16 * i)
                sp.dma_start(x_all[:, ds((2 * i + q) * BATCH, BATCH), :], x[ds((2 * i + q) * BATCH * P, BATCH * P), :]
                             .rearrange("(t p) d -> p t d", p=P)).then_inc(x_in[q], 16)

            def store_batch(i, q):
                b = 2 * i + q
                sp.wait_ge(m_relu, b + 1)
                sp.dma_start(table[ds(b * BATCH * P, BATCH * P), :].rearrange("(t p) d -> p t d", p=P),
                             rb[:, q, :, :]).then_inc(r_out[q], 16)

            load_edges(src, src_raw, src_pad, src_in)
            load_x(0, 0)
            for k, m in enumerate(weights):
                sp.dma_start(w_nat[:, k, :], m).then_inc(w_in, 16)
            load_x(0, 1)
            load_edges(dst, dst_raw, dst_pad, dst_in)
            load_x(1, 0)
            load_x(1, 1)
            for k, v in enumerate(vectors):
                sp.dma_start(vec[:, k:k + 1], v.rearrange("(p o) -> p o", o=1)).then_inc(vec_in, 16)
            AHEAD = 4
            with sp.Fori(2, AHEAD) as i:
                for q in range(2):
                    load_x(i, q)
            with sp.Fori(0, NB // 2 - AHEAD - 1) as i:
                for q in range(2):
                    store_batch(i, q)
                    load_x(i + AHEAD, q)
            i = NB // 2 - AHEAD - 1
            store_batch(i, 0)
            load_x(NB // 2 - 1, 0)
            store_batch(i, 1)
            sp.wait_ge(x_in[1], 16 * (NB // 2 - 1))
            sp.wait_ge(x_pad, 1)
            sp.dma_start(x_all[:, NT - BATCH:NT - 1, :], x[(NT - BATCH) * P:(NT - 1) * P, :]
                         .rearrange("(t p) d -> p t d", p=P)).then_inc(x_in[1], 16)
            sp.dma_start(x_all[0:LAST, NT - 1, :], x[(NT - 1) * P:N, :]).then_inc(x_in[1], 16)
            with sp.Fori(NB // 2 - AHEAD, NB // 2) as i:
                for q in range(2):
                    store_batch(i, q)

            def load_tile(t, q):
                sp.dma_start(xn[:, q, :], x[ds(t * P, P), :]).then_inc(xn_in[q], 16)

            def store_tile(t, q, last=False):
                rows = LAST if last else P
                sp.wait_ge(u_res, t + 1)
                sp.dma_start(out[ds(t * P, rows), :], res[0:rows, q, :]).then_inc(res_out[q], 16)

            sp.wait_ge(flag_set, 1)
            flag = sp.value_load(flag_i[0:1, 0:1], min_val=0, max_val=1)
            with sp.If(flag != 0):
                sp.dma_start(drow[:, :], dst[0:P].rearrange("(o e) -> o e", o=1)).then_inc(g_row, 16)
                with sp.Fori(1, FULL) as j:
                    sp.wait_ge(g_sum, j)
                    sp.dma_start(drow[:, :], dst[ds(j * P, P)].rearrange("(o e) -> o e", o=1)).then_inc(g_row, 16)
                sp.wait_ge(g_sum, FULL)
                sp.dma_start(drow[:, 0:TAIL], dst[FULL * P:E].rearrange("(o e) -> o e", o=1)).then_inc(g_row, 16)

            load_tile(0, 0)
            load_tile(1, 1)
            with sp.Fori(0, NT // 2 - 2) as i:
                for q in range(2):
                    store_tile(2 * i + q, q)
                    sp.wait_ge(res_out[q], 16 * (i + 1))
                    load_tile(2 * i + q + 2, q)
            sp.wait_ge(x_src_in, 16 * NR)
            sp.dma_start(x_last[:, 0, :], x[(NT - 2) * P:(NT - 1) * P, :]).then_inc(x_last_in, 16)
            sp.dma_start(x_last[0:LAST, 1, :], x[(NT - 1) * P:N, :]).then_inc(x_last_in, 16)
            for t in range(NT - 4, NT):
                store_tile(t, t % 2, last=t == NT - 1)
            for q in range(2):
                sp.wait_ge(res_out[q], 16 * (NT // 2))

        @block.gpsimd
        def _(pool):
            nc.gpsimd.memset(src_raw[:, EB - 1, :], 0).then_inc(src_pad, 1)
            nc.gpsimd.memset(ident[:, :], 0.0).then_inc(ident_zero, 1)
            pool.wait_ge(ident_zero, 1)
            nc.gpsimd.affine_select(out=ident[:, :], in_=ident[:, :], compare_op=ALU.not_equal, fill=1.0, base=0,
                                    pattern=[[-1, P]], channel_multiplier=1).then_inc(consts, 1)
            nc.gpsimd.iota(win[:, :], pattern=[[1, WIN]], base=0, channel_multiplier=0,
                           allow_small_or_imprecise_dtypes=True).then_inc(consts, 1)
            nc.gpsimd.iota(least[:, :], pattern=[[P, NG]], base=-P, channel_multiplier=0,
                           allow_small_or_imprecise_dtypes=True).then_inc(consts, 1)

            nc.gpsimd.memset(x_all[:, NT - 1, :], 0.0).then_inc(x_pad, 1)

            pool.wait_ge(first_in, 16)
            for r in range(NR):
                if r == NR0:
                    pool.wait_ge(idx_set, 1)
                index = idx_first[:, r:r + 1] if r < NR0 else idx[:, r * TPG + RAW:r * TPG + RAW + 1]
                nc.gpsimd.indirect_dma_start(
                    out=x_src[:, r, :], out_offset=None, in_=x,
                    in_offset=bass.IndirectOffsetOnAxis(ap=index, axis=0)).then_inc(x_src_in, 16)
            pool.wait_ge(flag_set, 1)
            for q in range(2):
                pool.wait_ge(r_out[q], 16 * (NB // 2))
            flag = pool.value_load(flag_i[0:1, 0:1], min_val=0, max_val=1)

            def gather(q, k, index):
                return nc.gpsimd.indirect_dma_start(
                    out=gat[:, q, k, :], out_offset=None, in_=table,
                    in_offset=bass.IndirectOffsetOnAxis(ap=index, axis=0))

            def gather_group(i, q, first, tiles=RAW):
                pool.wait_ge(idx_ready, 2 * i + q + 1)
                if not first:
                    pool.wait_ge(group_used, 2 * i + q - 1)
                pool.sem_inc(gathers_begun, 1)
                for k in range(tiles):
                    gather(q, k, idx_now[:, q, k:k + 1]).then_inc(got[q][k], 16)

            with pool.If(flag == 0):
                for q in range(2):
                    gather_group(0, q, True)
                with pool.Fori(1, NG // 2 - 1) as i:
                    for q in range(2):
                        gather_group(i, q, False)
                gather_group(NG // 2 - 1, 0, False)
                gather_group(NG // 2 - 1, 1, False, LASTK)
            with pool.Else():
                def gather_tile(j, first):
                    pool.wait_ge(g_idx, j + 1)
                    if not first:
                        pool.wait_ge(g_turned, j)
                    pool.sem_inc(gathers_begun, 1)
                    gather(0, 0, idx_now[:, 0, 0:1]).then_inc(g_got, 16)

                gather_tile(0, True)
                with pool.Fori(1, ET) as j:
                    gather_tile(j, False)

        @block.tensor
        def _(pe):
            pe.wait_ge(consts, 5)
            pe.wait_ge(src_cast, 1)

            def turn_edges(f, turned):
                for b in range(EB):
                    last = nc.tensor.transpose(flat[:, b * P:(b + 1) * P], f[:, b, :], ident[:, :])
                last.then_inc(turned, 1)

            turn_edges(src_f, src_turned)
            pe.wait_ge(w_in, 16 * len(weights))
            for k in range(len(weights)):
                last = nc.tensor.transpose(flat[:, 2048 + k * P:2048 + (k + 1) * P], w_nat[:, k, :], ident[:, :])
            last.then_inc(w_turned, 1)
            pe.wait_ge(idx_set, 1)
            pe.wait_ge(w_set, 1)

            def turn_h(i, q):
                b = 2 * i + q
                pe.wait_ge(m_h, b + 1)
                if not (isinstance(i, int) and b < 2):
                    pe.wait_ge(m_hTs, b - 1)
                for k in range(BATCH):
                    last = nc.tensor.transpose(psT[q][:, k * P:(k + 1) * P], hb[:, q, k, :], ident[:, :])
                last.then_inc(m_hT, 1)

            def multiply_h(i, q):
                b = 2 * i + q
                pe.wait_ge(m_hTs, b + 1)
                if not (isinstance(i, int) and b < 2):
                    pe.wait_ge(m_relu, b - 1)
                for k in range(BATCH):
                    last = nc.tensor.matmul(psR[q][:, k * P:(k + 1) * P], hTb[:, q, k * P:(k + 1) * P], W1aT,
                                            start=True, stop=True)
                last.then_inc(m_r, 1)

            for q in range(2):
                turn_h(0, q)
                multiply_h(0, q)
            with pe.Fori(1, NB // 2) as i:
                for q in range(2):
                    turn_h(i, q)
                    multiply_h(i, q)
            pe.wait_ge(m_relu, NB)
            pe.wait_ge(dst_cast, 1)
            turn_edges(dst_f, dst_turned)
            pe.wait_ge(dst_set, 1)
            for c, (first, _) in enumerate(CHUNKS):
                last = nc.tensor.matmul(ps[:, 6, c * NG:(c + 1) * NG], ones[0:1, :],
                                        key[0:1, first:NG * TPG:TPG], start=True, stop=True)
            last.then_inc(base_sent, 1)
            pe.wait_ge(bad_set, 1)
            nc.tensor.matmul(ps[0:1, 7, 0:1], ones[:, 0:1], bad[:, 3:4], start=True, stop=True).then_inc(bad_summed, 1)
            pe.wait_ge(diag_set, 2)
            pe.wait_ge(flag_set, 1)

            def sums(t, q):
                pe.wait_ge(u_sums, 2 * t + 2)
                nc.tensor.matmul(pSum[bank(t, q)], sum_now[:, q, :], W1bT, start=True, stop=True)
                nc.tensor.matmul(pCnt[bank(t, q)], cnt_now[:, q, :], ones[0:1, 0:1], start=True, stop=True).then_inc(u_raw, 1)

            def turn_node_h(t, q):
                pe.wait_ge(u_h, t + 1)
                nc.tensor.transpose(pH[bank(t, q)], hn[:, q, :], ident[:, :]).then_inc(u_hT, 1)

            def turn_agg(t, q):
                pe.wait_ge(u_z1, t + 1)
                pe.wait_ge(u_hTs, t + 1)
                nc.tensor.transpose(pZ1[bank(t, q)], z1[:, q, :], ident[:, :]).then_inc(u_z1T, 1)

            def mix(t, q):
                pe.wait_ge(u_hTs, t + 1)
                pe.wait_ge(u_aT, t + 1)
                nc.tensor.matmul(pY[bank(t, q)], hT[:, q, :], diag_h[:, :], start=True, stop=False)
                nc.tensor.matmul(pY[bank(t, q)], aT[:, q, :], diag_a[:, :], start=False, stop=True).then_inc(u_y, 1)

            def turn_fx(t, q):
                pe.wait_ge(u_z2, t + 1)
                nc.tensor.transpose(pZ2[bank(t, q)], z2[:, q, :], ident[:, :]).then_inc(u_z2T, 1)

            def hidden(t, q):
                pe.wait_ge(u_fT, t + 1)
                nc.tensor.matmul(pHid[bank(t, q)], W2fT, fT[:, q, :], start=True, stop=False)
                nc.tensor.matmul(pHid[bank(t, q)], W2gT, aT[:, q, :], start=False, stop=True).then_inc(u_hid, 1)

            def project(t, q):
                pe.wait_ge(u_hids, t + 1)
                nc.tensor.matmul(pOut[bank(t, q)], hid[:, q, :], W2bT, start=True, stop=True).then_inc(u_o, 1)

            steps = {0: sums, 1: turn_node_h, 3: turn_agg, 6: mix, 9: turn_fx, 11: hidden, 14: project}

            def turn_raw(g):
                pe.wait_ge(e_hs, g + 1)
                nc.tensor.transpose(pEh, e_h[:, :], ident[:, :]).then_inc(e_turned, 1)

            def multiply_raw(g):
                pe.wait_ge(e_copied, g + 1)
                nc.tensor.matmul(pEr, e_hT[:, :], W1aT, start=True, stop=True).then_inc(e_made, 1)

            raw_steps = {12: turn_raw, 15: multiply_raw}

            def group(i, q, first=False, nodes=1, tiles=TPG, plan=None):
                g = 2 * i + q
                pe.wait_ge(hot_ready, g + 1)
                if not first:
                    pe.wait_ge(sums_done, NC * (g - 1))
                    pe.wait_ge(cnts_done, NC * (g - 1))
                nc.tensor.matmul(psC[q], ones[:, 0:1], hot_sum[:, q, :, :].rearrange("p c w -> p (c w)"),
                                 start=True, stop=True)
                for c, (k0, n) in enumerate(CHUNKS):
                    for k in range(k0, min(k0 + n, tiles)):
                        if k == RAW:
                            pe.wait_ge(e_msg, g + 1)
                        else:
                            pe.wait_ge(got[q][k], 16 * (i + 1))
                        last = nc.tensor.matmul(psS[q][:, c * WIN:(c + 1) * WIN], gat[:, q, k, :], hot[:, q, k, :],
                                                start=k == k0, stop=k == k0 + n - 1)
                        if k == tiles - 1:
                            last.then_inc(group_used, 1)
                        if plan:
                            for f, t, p in plan.get(k, ()):
                                f(t, p)
                        elif nodes and k in steps:
                            steps[k](g - 3, 1 - q)
                        if tiles == TPG and k in raw_steps and not (isinstance(g, int) and g + 1 == NR):
                            raw_steps[k](g + 1)

            flag = pe.value_load(flag_i[0:1, 0:1], min_val=0, max_val=1)
            with pe.If(flag == 0):
                turn_raw(0)
                multiply_raw(0)
                group(0, 0, first=True, nodes=0)
                group(0, 1, first=True, nodes=0)
                group(1, 0, nodes=0)
                group(1, 1)
                with pe.Fori(2, NG // 2 - 1) as i:
                    for q in range(2):
                        group(i, q)
                group(NG // 2 - 1, 0)
                n4, n3, n2, n1 = ((NT - n, n % 2) for n in (4, 3, 2, 1))
                plan = {0: ((sums, *n4), (turn_node_h, *n4)), 2: ((turn_agg, *n4),), 3: ((mix, *n4),),
                        4: ((sums, *n3), (turn_node_h, *n3)), 6: ((turn_fx, *n4),),
                        8: ((hidden, *n4), (turn_agg, *n3))}
                group(NG // 2 - 1, 1, tiles=LASTK, plan=plan)
                project(*n4)
                mix(*n3)
                turn_node_h(*n2)
                sums(*n2)
                sums(*n1)
                turn_node_h(*n1)
                turn_fx(*n3)
                turn_agg(*n2)
                hidden(*n3)
                turn_agg(*n1)
                mix(*n2)
                project(*n3)
                mix(*n1)
                turn_fx(*n2)
                turn_fx(*n1)
                hidden(*n2)
                hidden(*n1)
                project(*n2)
                project(*n1)
            with pe.Else():
                def turn_tile(j, first):
                    pe.wait_ge(g_got, 16 * (j + 1))
                    if not first:
                        pe.wait_ge(g_copied, j)
                    nc.tensor.transpose(ps[:, 0, 0:P], gat[:, 0, 0, :], ident[:, :]).then_inc(g_turned, 1)

                turn_tile(0, True)
                with pe.Fori(1, ET) as j:
                    turn_tile(j, False)
                with pe.Fori(0, NT // 2 - 1) as i:
                    for q in range(2):
                        for f in steps.values():
                            f(2 * i + q, q)
                for q in range(2):
                    for f in steps.values():
                        f(NT - 2 + q, q)

        @block.scalar
        def _(act):
            act.wait_ge(consts, 5)

            def std(i, q):
                b = 2 * i + q
                act.wait_ge(m_var, b + 1)
                nc.scalar.activation(sd1[:, q, :], var1[:, q, :], ACT.Sqrt, bias=eps[:, 0:1]).then_inc(m_std, 1)

            def normalise(i, q):
                b = 2 * i + q
                act.wait_ge(m_norm, b + 1)
                if not (isinstance(i, int) and b < 2):
                    act.wait_ge(m_hT, b - 1)
                for k in range(BATCH):
                    t = b * BATCH + k
                    last = nc.scalar.activation(hb[:, q, k, :], cnt_rows[:, ds(t * D, D)], ACT.Relu,
                                                scale=rs_all[:, ds(t, 1)], bias=nm_all[:, ds(t, 1)])
                last.then_inc(m_h, 1)

            def relu(i, q):
                b = 2 * i + q
                act.wait_ge(m_r, b + 1)
                if not (isinstance(i, int) and b < 2):
                    act.wait_ge(r_out[q], 16 * i)
                nc.scalar.activation(rb[:, q, :, :].rearrange("p t d -> p (t d)"), psR[q], ACT.Relu).then_inc(m_relu, 1)

            std(0, 0)
            normalise(0, 0)
            std(0, 1)
            normalise(0, 1)
            std(1, 0)
            for q in range(2):
                normalise(1, q)
                std(1 + q, 1 - q)
                relu(0, q)
            with act.Fori(2, NB // 2 - 1) as i:
                for q in range(2):
                    normalise(i, q)
                    std(i + q, 1 - q)
                    relu(i - 1, q)
            i = NB // 2 - 1
            normalise(i, 0)
            std(i, 1)
            relu(i - 1, 0)
            normalise(i, 1)
            relu(i - 1, 1)
            relu(i, 0)
            relu(i, 1)

            def take_sums(t, q, i):
                nc.scalar.copy(sum_now[:, q, :], acc[:, ds(t * P, P)]).then_inc(u_sums, 1)
                nc.scalar.copy(cnt_now[:, q, :], cnt[:, ds(t * P, P)]).then_inc(u_sums, 1)

            def take_after(added, *nodes):
                act.wait_ge(sums_done, added)
                act.wait_ge(cnts_done, added)
                for node in nodes:
                    take_sums(*node)

            def node_h(t, q, i):
                if late(t):
                    act.wait_ge(x_last_in, 32)
                else:
                    act.wait_ge(xn_in[q], 16 * (i + 1))
                nc.scalar.activation(hn[:, q, :], x_of(t, q), ACT.Relu, scale=rs_all[:, ds(t, 1)],
                                     bias=nm_all[:, ds(t, 1)]).then_inc(u_h, 1)

            def keep_node_h(t, q, i):
                act.wait_ge(u_hT, t + 1)
                nc.scalar.copy(hT[:, q, :], pH[bank(t, q)]).then_inc(u_hTs, 1)

            def std_sum(t, q, i):
                act.wait_ge(u_small, 3 * t + 3)
                nc.scalar.activation(small[:, q, 3:4], small[:, q, 2:3], ACT.Sqrt).then_inc(u_std, 1)

            def scale_agg(t, q, i):
                act.wait_ge(u_z1T, t + 1)
                nc.scalar.activation(aT[:, q, :], pZ1[bank(t, q)], ACT.Identity, scale=vec[:, 0:1],
                                     bias=vec[:, 1:2]).then_inc(u_aT, 1)

            def std_mix(t, q, i):
                act.wait_ge(u_var2, t + 1)
                nc.scalar.activation(small[:, q, 5:6], mv3[:, q, 1:2], ACT.Sqrt, bias=eps[:, 0:1]).then_inc(u_std2, 1)

            def scale_fx(t, q, i):
                act.wait_ge(u_z2T, t + 1)
                nc.scalar.activation(fT[:, q, :], pZ2[bank(t, q)], ACT.Identity, scale=vec[:, 3:4],
                                     bias=vec[:, 4:5]).then_inc(u_fT, 1)

            def relu_hidden(t, q, i):
                act.wait_ge(u_hid, t + 1)
                nc.scalar.activation(hid[:, q, :], pHid[bank(t, q)], ACT.Relu).then_inc(u_hids, 1)

            def raw_std(g):
                act.wait_ge(e_var, g + 1)
                nc.scalar.activation(e_sc[:, 0:1], e_mv[:, 1:2], ACT.Sqrt, bias=eps[:, 0:1]).then_inc(e_std, 1)

            def raw_h(g):
                act.wait_ge(e_norm, g + 1)
                nc.scalar.activation(e_h[:, :], x_src[:, ds(g, 1), :].rearrange("p o d -> p (o d)"), ACT.Relu,
                                     scale=e_sc[:, 1:2], bias=e_sc[:, 2:3]).then_inc(e_hs, 1)

            def raw_keep(g):
                act.wait_ge(e_turned, g + 1)
                nc.scalar.copy(e_hT[:, :], pEh).then_inc(e_copied, 1)

            def raw_relu(g, q, first):
                act.wait_ge(e_made, g + 1)
                if not first:
                    act.wait_ge(group_used, g - 1)
                nc.scalar.activation(gat[:, q, RAW, :], pEr, ACT.Relu).then_inc(e_msg, 1)

            update = (node_h, std_sum, keep_node_h, scale_agg, std_mix, scale_fx, relu_hidden)

            def group(i, q, nodes=1, raws=1, take=1):
                g = 2 * i + q
                node = (g - 3, 1 - q, i - 2 + q)
                if nodes:
                    for f in update:
                        f(*node)
                if raws:
                    raw_std(g + 1)
                    raw_h(g + 1)
                if take:
                    take_after(NC * g, (g - 2, q, i - 1))
                if raws:
                    raw_keep(g + 1)
                    raw_relu(g + 1, 1 - q, False)

            act.wait_ge(vec_in, 16 * len(vectors))
            act.wait_ge(flag_set, 1)
            flag = act.value_load(flag_i[0:1, 0:1], min_val=0, max_val=1)
            with act.If(flag == 0):
                raw_std(0)
                raw_h(0)
                raw_keep(0)
                raw_relu(0, 0, True)
                raw_std(1)
                raw_h(1)
                raw_keep(1)
                raw_relu(1, 1, True)
                group(0, 1, nodes=0, take=0)
                group(1, 0, nodes=0)
                group(1, 1)
                with act.Fori(2, NG // 2 - 1) as i:
                    for q in range(2):
                        group(i, q)
                group(NG // 2 - 1, 0, raws=0)
                n4, n3, n2, n1 = ((NT - n, n % 2, (NT - n) // 2) for n in (4, 3, 2, 1))
                node_h(*n4)
                std_sum(*n4)
                keep_node_h(*n4)
                scale_agg(*n4)
                node_h(*n3)
                take_after(NC * (NG - 1), n3)
                std_mix(*n4)
                keep_node_h(*n3)
                scale_fx(*n4)
                std_sum(*n3)
                scale_agg(*n3)
                relu_hidden(*n4)
                node_h(*n2)
                node_h(*n1)
                take_after(NC * (NG - 1) + sum(k0 < LASTK for k0, _ in CHUNKS), n2, n1)
                keep_node_h(*n2)
                std_mix(*n3)
                std_sum(*n2)
                keep_node_h(*n1)
                std_sum(*n1)
                scale_fx(*n3)
                scale_agg(*n2)
                relu_hidden(*n3)
                scale_agg(*n1)
                std_mix(*n2)
                std_mix(*n1)
                scale_fx(*n2)
                scale_fx(*n1)
                relu_hidden(*n2)
                relu_hidden(*n1)
            with act.Else():
                act.wait_ge(g_sum, ET)
                with act.Fori(0, NT // 2 - 1) as i:
                    for q in range(2):
                        for f in (take_sums,) + update:
                            f(2 * i + q, q, i)
                for q in range(2):
                    for f in (take_sums,) + update:
                        f(NT - 2 + q, q, NT // 2 - 1)

        @block.vector
        def _(dve):
            nc.vector.memset(ones[:, :], 1.0).then_inc(consts, 1)
            nc.vector.memset(eps[:, :], EPS).then_inc(consts, 1)
            nc.vector.memset(dst_raw[:, EB - 1, :], N).then_inc(dst_pad, 1)
            nc.vector.memset(idx[:, EB * P:], 0)
            nc.vector.memset(key[:, EB * P:NG * TPG], float(N))
            nc.vector.memset(key[:, NG * TPG:], 0.0)
            dve.wait_ge(src_in, 48)
            nc.vector.tensor_copy(src_f[:, :, :], src_raw[:, :, :]).then_inc(src_cast, 1)
            dve.wait_ge(src_turned, 1)
            nc.vector.tensor_copy(idx[:, 0:EB * P], flat[:, 0:EB * P]).then_inc(idx_set, 1)
            dve.wait_ge(w_turned, 1)
            nc.vector.tensor_copy(w_T[:, :, :].rearrange("p k d -> p (k d)"),
                                  flat[:, 2048:2048 + 5 * P]).then_inc(w_set, 1)

            def find_keys():
                dve.wait_ge(dst_turned, 1)
                nc.vector.tensor_copy(key[:, 0:EB * P], flat[:, 0:EB * P]).then_inc(dst_set, 1)
                dve.wait_ge(base_sent, 1)
                nc.vector.tensor_copy(base_b[:, :, :].rearrange("p g c -> p c g"),
                                      ps[:, 6, 0:NC * NG].rearrange("p (c g) -> p c g", c=NC)).then_inc(prep, 1)
                dve.wait_ge(prep, 1)
                dve.wait_ge(dst_set, 1)
                nc.vector.tensor_copy(base_i[:, :], base_b[0:1, :, :].rearrange("p g c -> p (g c)")).then_inc(prep, 1)
                by_group = key[:, 0:NG * TPG].rearrange("p (g k) -> p g k", k=TPG)
                for c, (k0, n) in enumerate(CHUNKS):
                    nc.vector.tensor_tensor(by_group[:, :, k0:k0 + n], by_group[:, :, k0:k0 + n],
                                            base_b[:, :, c:c + 1].broadcast_to([P, NG, n]), ALU.subtract).then_inc(prep, 1)
                nc.vector.tensor_tensor(slack[:, :, :], base_b[:, :, :],
                                        least[:, :].unsqueeze(2).broadcast_to([P, NG, NC]), ALU.subtract).then_inc(prep, 1)
                dve.wait_ge(prep, 6)
                nc.vector.tensor_reduce(bad[:, 0:1], key[:, 0:NG * TPG], AX.X, ALU.max).then_inc(prep, 1)
                nc.vector.tensor_reduce(bad[:, 1:2], key[:, 0:NG * TPG], AX.X, ALU.min).then_inc(prep, 1)
                nc.vector.tensor_reduce(bad[:, 2:3], slack[:, :, :], AX.XY, ALU.min).then_inc(prep, 1)
                dve.wait_ge(prep, 9)
                nc.vector.tensor_scalar(bad[:, 3:4], bad[:, 0:1], float(WIN), None, ALU.is_ge).then_inc(prep, 1)
                for m in (1, 2):
                    dve.wait_ge(prep, 9 + m)
                    last = nc.vector.scalar_tensor_tensor(out=bad[:, 3:4], in0=bad[:, m:m + 1], scalar=0.0,
                                                          in1=bad[:, 3:4], op0=ALU.is_lt, op1=ALU.add)
                    last.then_inc(prep if m == 1 else bad_set, 1)
                dve.wait_ge(bad_summed, 1)
                nc.vector.tensor_copy(pWin, win[:, :]).then_inc(win_set, 1)
                nc.vector.tensor_scalar(flag_i[:, :], ps[0:1, 7, 0:1], 1.0, None, ALU.min).then_inc(flag_set, 1)

            def set_diagonals():
                dve.wait_ge(vec_in, 16 * len(vectors))
                dve.wait_ge(consts, 5)
                nc.vector.tensor_scalar(vec2[:, 0:1], vec[:, 2:3], 1.0, None, ALU.add).then_inc(vec_set, 1)
                nc.vector.tensor_scalar(vec2[:, 1:2], vec[:, 2:3], -1.0, None, ALU.mult).then_inc(vec_set, 1)
                dve.wait_ge(vec_set, 2)
                nc.vector.tensor_scalar(diag_h[:, :], ident[:, :], vec2[:, 0:1], None, ALU.mult).then_inc(diag_set, 1)
                nc.vector.tensor_scalar(diag_a[:, :], ident[:, :], vec2[:, 1:2], None, ALU.mult).then_inc(diag_set, 1)

            def spreads(i, q, extra=0):
                b = 2 * i + q
                dve.wait_ge(x_in[q], 16 * (i + 1) + extra)
                for k in range(BATCH):
                    last = nc.vector.bn_stats(st1[:, q, k, :], cnt_rows[:, ds((b * BATCH + k) * D, D)])
                last.then_inc(m_stats, 1)
                dve.wait_ge(m_stats, b + 1)
                ev, od = st1[:, q, :, 0:3], st1[:, q, :, 3:6]
                nc.vector.tensor_tensor(mean2[:, q, :], ev[:, :, 1], od[:, :, 1], ALU.add)
                nc.vector.tensor_tensor(apart[:, q, :], ev[:, :, 1], od[:, :, 1], ALU.subtract)
                nc.vector.tensor_tensor(spread[:, q, :], ev[:, :, 2], od[:, :, 2], ALU.add).then_inc(m_joined, 1)
                dve.wait_ge(m_joined, 2 * b + 1)
                nc.vector.scalar_tensor_tensor(out=apart2[:, q, :], in0=apart[:, q, :], scalar=0.25, in1=apart[:, q, :],
                                               op0=ALU.mult, op1=ALU.mult).then_inc(m_joined, 1)
                dve.wait_ge(m_joined, 2 * b + 2)
                nc.vector.scalar_tensor_tensor(out=var1[:, q, :], in0=spread[:, q, :], scalar=1.0 / D, in1=apart2[:, q, :],
                                               op0=ALU.mult, op1=ALU.add).then_inc(m_var, 1)

            def scales(i, q):
                b = 2 * i + q
                dve.wait_ge(m_std, b + 1)
                nc.vector.reciprocal(rs_all[:, ds(b * BATCH, BATCH)], sd1[:, q, :]).then_inc(m_rstd, 1)
                dve.wait_ge(m_rstd, b + 1)
                nc.vector.scalar_tensor_tensor(out=nm_all[:, ds(b * BATCH, BATCH)], in0=mean2[:, q, :], scalar=-0.5,
                                               in1=rs_all[:, ds(b * BATCH, BATCH)],
                                               op0=ALU.mult, op1=ALU.mult).then_inc(m_norm, 1)

            def keep_h(i, q):
                b = 2 * i + q
                dve.wait_ge(m_hT, b + 1)
                if not (isinstance(i, int) and b < 2):
                    dve.wait_ge(m_r, b - 1)
                nc.vector.tensor_copy(hTb[:, q, :], psT[q]).then_inc(m_hTs, 1)

            for q in range(2):
                spreads(0, q)
                scales(0, q)
            for q in range(2):
                spreads(1, q)
                keep_h(0, q)
                scales(1, q)
            with dve.Fori(2, NB // 2 - 1) as i:
                for q in range(2):
                    spreads(i, q)
                    keep_h(i - 1, q)
                    scales(i, q)
            i = NB // 2 - 1
            for q in range(2):
                spreads(i, q, extra=16 * q)
                keep_h(i - 1, q)
                scales(i, q)
            for q in range(2):
                keep_h(i, q)
            dve.wait_ge(dst_in, 48)
            nc.vector.tensor_copy(dst_f[:, :, :], dst_raw[:, :, :]).then_inc(dst_cast, 1)
            set_diagonals()
            find_keys()

            def ready_indices(i, q, first=False):
                g = 2 * i + q
                if not first:
                    dve.wait_ge(group_used, g - 1)
                nc.vector.tensor_copy(idx_now[:, q, :], idx[:, ds(g * TPG, TPG)]).then_inc(idx_ready, 1)

            def ready_hot(i, q):
                g = 2 * i + q
                nc.vector.tensor_tensor(hot[:, q, :, :], pWin.unsqueeze(1).broadcast_to([P, TPG, WIN]),
                                        key[:, ds(g * TPG, TPG)].unsqueeze(2).broadcast_to([P, TPG, WIN]),
                                        ALU.is_equal).then_inc(hot_made, 1)

            def ready_counts(i, q):
                dve.wait_ge(hot_made, 2 * i + q + 1)
                for c, (k0, n) in enumerate(CHUNKS):
                    last = nc.vector.tensor_reduce(hot_sum[:, q, c, :], hot[:, q, k0:k0 + n, :].rearrange("p k w -> p w k"),
                                                   AX.X, ALU.add)
                last.then_inc(hot_ready, 1)

            def ready_group(i, q, first):
                ready_indices(i, q, first)
                ready_hot(i, q)
                ready_counts(i, q)

            def load_bases(i, q, chunks=NC):
                return [dve.value_load(base_i[0:1, ds((2 * i + q) * NC + c, 1)], min_val=0, max_val=N)
                        for c in range(chunks)]

            def add_group(i, q, bases):
                g = 2 * i + q
                dve.wait_ge(group_used, g + 1)
                for c, at in enumerate(bases):
                    dve.wait_ge(sums_done, g * NC + c)
                    nc.vector.tensor_tensor(acc[:, ds(at, WIN)], acc[:, ds(at, WIN)],
                                            psS[q][:, c * WIN:(c + 1) * WIN], ALU.add).then_inc(sums_done, 1)
                    dve.wait_ge(cnts_done, g * NC + c)
                    nc.vector.tensor_tensor(cnt[:, ds(at, WIN)], cnt[:, ds(at, WIN)],
                                            psC[q][:, c * WIN:(c + 1) * WIN], ALU.add).then_inc(cnts_done, 1)

            def raw_stats(g):
                nc.vector.bn_stats(e_st[:, :], x_src[:, ds(g, 1), :].rearrange("p o d -> p (o d)"))
                dve.drain()
                nc.vector.bn_aggr(e_mv[:, :], e_st[:, :]).then_inc(e_var, 1)
                dve.wait_ge(e_std, g + 1)
                nc.vector.reciprocal(e_sc[:, 1:2], e_sc[:, 0:1]).then_inc(e_rstd, 1)
                dve.wait_ge(e_var, g + 1)
                dve.wait_ge(e_rstd, g + 1)
                nc.vector.scalar_tensor_tensor(out=e_sc[:, 2:3], in0=e_mv[:, 0:1], scalar=-1.0, in1=e_sc[:, 1:2],
                                               op0=ALU.mult, op1=ALU.mult).then_inc(e_norm, 1)

            def agg_stats(t, q, i):
                dve.wait_ge(u_raw, t + 1)
                nc.vector.bn_stats(st2[:, q, :], pSum[bank(t, q)])
                nc.vector.tensor_scalar(small[:, q, 0:1], pCnt[bank(t, q)], 1.0, None, ALU.max).then_inc(u_small, 1)
                dve.wait_ge(u_small, 3 * t + 1)
                nc.vector.scalar_tensor_tensor(out=small[:, q, 1:2], in0=small[:, q, 0:1], scalar=EPS,
                                               in1=small[:, q, 0:1], op0=ALU.mult, op1=ALU.mult).then_inc(u_small, 1)
                dve.drain()
                nc.vector.bn_aggr(mv2[:, q, :], st2[:, q, :]).then_inc(u_var, 1)
                dve.wait_ge(u_small, 3 * t + 2)
                dve.wait_ge(u_var, t + 1)
                nc.vector.tensor_tensor(small[:, q, 2:3], small[:, q, 1:2], mv2[:, q, 1:2], ALU.add).then_inc(u_small, 1)

            def agg_norm(t, q, i):
                dve.wait_ge(u_std, t + 1)
                nc.vector.reciprocal(small[:, q, 4:5], small[:, q, 3:4]).then_inc(u_scale, 1)
                dve.wait_ge(u_scale, t + 1)
                nc.vector.tensor_scalar(z1[:, q, :], pSum[bank(t, q)], mv2[:, q, 0:1], small[:, q, 4:5],
                                        ALU.subtract, ALU.mult).then_inc(u_z1, 1)

            def mix_stats(t, q, i):
                dve.wait_ge(u_y, t + 1)
                nc.vector.bn_stats(st3[:, q, :], pY[bank(t, q)])
                dve.drain()
                nc.vector.bn_aggr(mv3[:, q, :], st3[:, q, :]).then_inc(u_var2, 1)

            def mix_norm(t, q, i):
                dve.wait_ge(u_std2, t + 1)
                nc.vector.reciprocal(small[:, q, 6:7], small[:, q, 5:6]).then_inc(u_scale2, 1)
                dve.wait_ge(u_scale2, t + 1)
                dve.wait_ge(u_var2, t + 1)
                nc.vector.tensor_scalar(z2[:, q, :], pY[bank(t, q)], mv3[:, q, 0:1], small[:, q, 6:7],
                                        ALU.subtract, ALU.mult).then_inc(u_z2, 1)

            def residual(t, q, i):
                dve.wait_ge(u_o, t + 1)
                if late(t):
                    dve.wait_ge(x_last_in, 32)
                    dve.wait_ge(res_out[q], 16 * i)
                else:
                    dve.wait_ge(xn_in[q], 16 * (i + 1))
                nc.vector.tensor_tensor(res[:, q, :], pOut[bank(t, q)], x_of(t, q), ALU.add).then_inc(u_res, 1)

            update = (agg_stats, agg_norm, mix_stats, mix_norm, residual)
            dve.wait_ge(flag_set, 1)
            flag = dve.value_load(flag_i[0:1, 0:1], min_val=0, max_val=1)

            for q in range(2):
                dve.wait_ge(r_out[q], 16 * (NB // 2))
            with dve.If(flag == 0):
                dve.wait_ge(win_set, 1)
                ready_group(0, 0, True)
                ready_group(0, 1, True)
                nc.vector.memset(acc[:, :], 0.0).then_inc(acc_zero, 1)
                dve.wait_ge(x_src_in, 16 * NR)
                raw_stats(0)
                raw_stats(1)
                nc.vector.memset(cnt[:, :], 0.0).then_inc(acc_zero, 1)
                dve.wait_ge(acc_zero, 2)
                add_group(0, 0, load_bases(0, 0))
                ready_group(1, 0, False)
                raw_stats(2)
                add_group(0, 1, load_bases(0, 1))
                ready_group(1, 1, False)
                raw_stats(3)

                def body(i, q):
                    g = 2 * i + q
                    node = (g - 3, 1 - q, i - 2 + q)
                    bases = load_bases(i - 1 + q, 1 - q)
                    ready_indices(i + q, 1 - q)
                    agg_stats(*node)
                    agg_norm(*node)
                    ready_hot(i + q, 1 - q)
                    mix_stats(*node)
                    mix_norm(*node)
                    if not (isinstance(g, int) and g + 1 >= NR):
                        raw_stats(g + 1)
                    add_group(i - 1 + q, 1 - q, bases)
                    ready_counts(i + q, 1 - q)
                    residual(*node)

                body(1, 1)
                with dve.Fori(2, NG // 2 - 1) as i:
                    for q in range(2):
                        body(i, q)
                body(NG // 2 - 1, 0)
                n4, n3, n2, n1 = ((NT - n, n % 2, (NT - n) // 2) for n in (4, 3, 2, 1))
                chunks = sum(k0 < LASTK for k0, _ in CHUNKS)
                agg_stats(*n4)
                bases = load_bases(NG // 2 - 1, 0)
                agg_norm(*n4)
                add_group(NG // 2 - 1, 0, bases)
                mix_stats(*n4)
                bases = load_bases(NG // 2 - 1, 1, chunks)
                mix_norm(*n4)
                agg_stats(*n3)
                agg_norm(*n3)
                add_group(NG // 2 - 1, 1, bases)
                residual(*n4)
                mix_stats(*n3)
                agg_stats(*n2)
                mix_norm(*n3)
                agg_stats(*n1)
                agg_norm(*n2)
                agg_norm(*n1)
                mix_stats(*n2)
                residual(*n3)
                mix_norm(*n2)
                mix_stats(*n1)
                mix_norm(*n1)
                residual(*n2)
                residual(*n1)
            with dve.Else():
                nc.vector.memset(acc[:, :], 0.0).then_inc(acc_zero, 1)
                nc.vector.memset(cnt[:, :], 0.0).then_inc(acc_zero, 1)
                dve.wait_ge(acc_zero, 2)

                def add_edges(j, n):
                    dve.wait_ge(g_row, 16 * (j + 1))
                    dve.wait_ge(g_turned, j + 1)
                    nc.vector.tensor_copy(gT[:, :], ps[:, 0, 0:P]).then_inc(g_copied, 1)
                    dve.drain()
                    with dve.Fori(0, n) as e:
                        at = dve.value_load(drow[0:1, ds(e, 1)], min_val=0, max_val=N - 1)
                        nc.vector.tensor_tensor(acc[:, ds(at, 1)], acc[:, ds(at, 1)], gT[:, ds(e, 1)], ALU.add)
                        nc.vector.tensor_tensor(cnt[:, ds(at, 1)], cnt[:, ds(at, 1)], ones[0:1, 0:1], ALU.add)
                        dve.drain()
                    dve.drain().then_inc(g_sum, 1)

                with dve.Fori(0, FULL) as j:
                    nc.vector.tensor_copy(idx_now[:, 0, 0:1], idx[:, ds(j, 1)]).then_inc(g_idx, 1)
                    add_edges(j, P)
                nc.vector.tensor_copy(idx_now[:, 0, 0:1], idx[:, FULL:FULL + 1]).then_inc(g_idx, 1)
                add_edges(FULL, TAIL)
                with dve.Fori(0, NT // 2 - 1) as i:
                    for q in range(2):
                        for f in update:
                            f(2 * i + q, q, i)
                for q in range(2):
                    for f in update:
                        f(NT - 2 + q, q, NT // 2 - 1)


_INS = ['x', 'src', 'dst', 'L0_gnn_W1a', 'L0_gnn_W1b', 'L0_gnn_ln1_g', 'L0_gnn_ln1_b', 'L0_gnn_w', 'L0_gnn_ln2_g',
        'L0_gnn_ln2_b', 'L0_gnn_W2a', 'L0_gnn_W2b']


def kernel(**inputs):
    import numpy as _np
    import concourse.bacc as _bacc
    from concourse import mybir as _mybir
    from concourse.bass_utils import run_bass_kernel_spmd as _run

    nc = _bacc.Bacc("TRN2", target_bir_lowering=False, num_devices=1)
    arrays, args = {}, []
    for name in _INS:
        a = _np.ascontiguousarray(inputs[name])
        arrays[f"in_{name}_dram"] = a
        args.append(nc.dram_tensor(f"in_{name}_dram", a.shape, _mybir.dt.from_np(a.dtype), kind="ExternalInput").ap())
    out = nc.dram_tensor("out_0_dram", inputs['x'].shape, _mybir.dt.float32, kind="ExternalOutput").ap()
    gnn_kernel(nc, *args, out)
    r = _run(nc, [arrays], core_ids=[0])
    return r.results[0]["out_0_dram"]
```
